# Optimizing a Trainium2 kernel written in Bass

```python
import numpy as np
import jax
import jax.numpy as jnp

def _softmax(x, axis=-1):
    return jax.nn.softmax(x, axis=axis)

def _gelu(x):
    return jax.nn.gelu(x, approximate=True)

def _silu(x):
    return jax.nn.silu(x)

def _sigmoid(x):
    return jax.nn.sigmoid(x)

def _layernorm(x, axis=-1, eps=1e-05):
    m = jnp.mean(x, axis=axis, keepdims=True)
    v = jnp.var(x, axis=axis, keepdims=True)
    return (x - m) / jnp.sqrt(v + eps)

def _scatter_add(tgt, idx, src, axis=0):
    return tgt.at[idx].add(src)

def _segment_sum(src, seg, n):
    return jax.ops.segment_sum(src, seg, n)
kernel_name = 'mk_cond_resid_d4_seqx_r8_aa4112'

def setup_inputs(seed: int=0):
    np.random.seed(seed)
    _w = jnp.asarray

    def _rec_inputs():
        import jax
        import jax.numpy as jnp
        _rk = jax.random.key(seed)
        x = -0.0005207 + 1.001 * jax.random.normal(jax.random.fold_in(_rk, 1), (32, 32, 512), jnp.float32)
        _lenS = 32 - jax.random.randint(jax.random.fold_in(_rk, 7), (32,), 0, max(1, 32 // 4) + 1, jnp.int32)
        _lenS2 = 32 - jax.random.randint(jax.random.fold_in(_rk, 8), (32,), 0, max(1, 32 // 4) + 1, jnp.int32)
        itok_Bx16_0_63 = jax.random.randint(jax.random.fold_in(_rk, 11), (32, 16), 0, 64, jnp.int32)
        itok_B_207_1644 = jax.random.randint(jax.random.fold_in(_rk, 12), (32,), 207, 1645, jnp.int32)
        itok_B_0_15 = jax.random.randint(jax.random.fold_in(_rk, 13), (32,), 0, 16, jnp.int32)
        condB_scale = 0.000342416 + 0.0128191 * jax.random.normal(jax.random.fold_in(_rk, 14), (32,), jnp.float32)
        itok_Bx4096x4096_0_255 = jax.random.randint(jax.random.fold_in(_rk, 15), (32, 512, 512), 0, 32, jnp.int32)
        condB_wscale = jax.random.uniform(jax.random.fold_in(_rk, 16), (32,), jnp.float32, 0.0, 0.00091742)
        itok_Bx4096_0_255 = jax.random.randint(jax.random.fold_in(_rk, 18), (32, 512), 0, 32, jnp.int32)
        condB_bscale = jax.random.uniform(jax.random.fold_in(_rk, 19), (32,), jnp.float32, 0.0, 0.000800939)
        itok_B_3_7 = jax.random.randint(jax.random.fold_in(_rk, 20), (32,), 3, 8, jnp.int32)
        return (x, itok_Bx16_0_63, itok_B_207_1644, itok_B_0_15, condB_scale, itok_Bx4096x4096_0_255, condB_wscale, itok_Bx4096_0_255, condB_bscale, itok_B_3_7, _lenS)
    x, itok_Bx16_0_63, itok_B_207_1644, itok_B_0_15, condB_scale, itok_Bx4096x4096_0_255, condB_wscale, itok_Bx4096_0_255, condB_bscale, itok_B_3_7, _lenS = _rec_inputs()

    def _L0_cond_setup():
        import jax, jax.numpy as jnp
        import numpy as np
        B, S, HID = (4, 128, 512)
        D, HQ, HK = (128, 32, 8)
        PAGES, PSIZE, NPP = (64, 32, 16)
        THETA = 10000.0
        EPS = 1e-06
        SCALE = 1.0 / float(np.sqrt(D))

        def _rmsnorm(t, w):
            var = jnp.mean(t * t, axis=-1, keepdims=True)
            return t * jax.lax.rsqrt(var + EPS) * w

        def _rope(t, pos):
            inv_freq = 1.0 / THETA ** (jnp.arange(0, D, 2, dtype=jnp.float32) / D)
            freqs = pos[..., None].astype(jnp.float32) * inv_freq
            cos = jnp.cos(freqs)[:, :, None, :]
            sin = jnp.sin(freqs)[:, :, None, :]
            t1, t2 = (t[..., :D // 2], t[..., D // 2:])
            return jnp.concatenate([t1 * cos - t2 * sin, t2 * cos + t1 * sin], axis=-1)
        key = jax.random.key(seed)
        ks = jax.random.split(key, 10)
        x = jax.random.normal(ks[0], (B, S, HID), jnp.float32)
        Wq = jax.random.normal(ks[1], (HQ * D, HID), jnp.float32) * 0.02
        Wk = jax.random.normal(ks[2], (HK * D, HID), jnp.float32) * 0.02
        Wv = jax.random.normal(ks[3], (HK * D, HID), jnp.float32) * 0.02
        Wo = jax.random.normal(ks[4], (HID, HQ * D), jnp.float32) * 0.02
        q_norm_w = jax.random.uniform(ks[5], (D,), jnp.float32)
        k_norm_w = jax.random.uniform(ks[6], (D,), jnp.float32)
        k_cache = jax.random.normal(ks[7], (PAGES, PSIZE, HK, D), jnp.float32)
        v_cache = jax.random.normal(ks[8], (PAGES, PSIZE, HK, D), jnp.float32)
        block_table = jnp.arange(B * NPP, dtype=jnp.int32).reshape(B, NPP)
        cache_seqlens = jax.random.randint(ks[9], (B,), 0, 475).astype(jnp.int32)
        return dict(x=x, Wq=Wq, Wk=Wk, Wv=Wv, Wo=Wo, q_norm_w=q_norm_w, k_norm_w=k_norm_w, k_cache=k_cache, v_cache=v_cache, block_table=block_table, cache_seqlens=cache_seqlens)
    _L0_cond_all = _L0_cond_setup()
    _L0_cond_in = {k: v for k, v in _L0_cond_all.items() if k in ('Wq', 'Wk', 'Wv', 'Wo', 'q_norm_w', 'k_norm_w', 'k_cache', 'v_cache')}
    del _L0_cond_all

    def _L1_cond_setup():
        import jax, jax.numpy as jnp
        import numpy as np
        NUM_CONDITIONS = 16
        IN_CH = 32
        OUT_CH = 32
        B = 64
        T = 512
        key = jax.random.key(seed)
        k_x, k_w, k_c = jax.random.split(key, 3)
        x = jax.random.normal(k_x, (B, IN_CH, T), dtype=jnp.float32)
        bound = float(np.sqrt(6.0 / IN_CH))
        weights = jax.random.uniform(k_w, (NUM_CONDITIONS, IN_CH, OUT_CH), dtype=jnp.float32, minval=-bound, maxval=bound)
        condition = jax.random.randint(k_c, (B,), 0, NUM_CONDITIONS, dtype=jnp.int64)
        return {'x': x, 'weights': weights, 'condition': condition}
    _L1_cond_all = _L1_cond_setup()
    _L1_cond_in = {k: v for k, v in _L1_cond_all.items() if k in ('weights',)}
    del _L1_cond_all

    def _L2_cond_setup():
        import jax, jax.numpy as jnp
        import numpy as np
        key = jax.random.key(seed)
        ks = jax.random.split(key, 10)
        N, OUT, IN = (8, 512, 512)
        B, S = (8, 256)
        return {'x': jax.random.normal(ks[0], (B, S, IN), dtype=jnp.float32), 'weight': jax.random.normal(ks[1], (OUT, IN), dtype=jnp.float32) * 0.02, 'bias': jax.random.normal(ks[2], (OUT,), dtype=jnp.float32) * 0.02, 'scale': jax.random.normal(ks[3], (N,), dtype=jnp.float32) * 0.01, 'wq': jax.random.randint(ks[4], (N, OUT, IN), 0, 32, dtype=jnp.int32), 'wscale': jax.random.uniform(ks[5], (N,), dtype=jnp.float32) * 0.001, 'wzp': jax.random.randint(ks[6], (N,), 0, 32, dtype=jnp.int32), 'bq': jax.random.randint(ks[7], (N, OUT), 0, 32, dtype=jnp.int32), 'bscale': jax.random.uniform(ks[8], (N,), dtype=jnp.float32) * 0.001, 'bzp': jax.random.randint(ks[9], (N,), 0, 32, dtype=jnp.int32)}
    _L2_cond_all = _L2_cond_setup()
    _L2_cond_in = {k: v for k, v in _L2_cond_all.items() if k in ('weight', 'bias')}
    del _L2_cond_all

    def _L3_cond_setup():
        import jax, jax.numpy as jnp
        import numpy as np
        RANK = 16
        ALPHA = 16.0
        SCALING = ALPHA / RANK
        N_ADAPTERS = 8
        IN_F = 512
        OUT_F = 512
        BATCH = 4
        SEQ = 256
        key = jax.random.key(seed)
        kx, ka, kb, ki = jax.random.split(key, 4)
        x = jax.random.normal(kx, (BATCH, SEQ, IN_F), dtype=jnp.float32)
        A = jax.random.normal(ka, (N_ADAPTERS, OUT_F, RANK), dtype=jnp.float32) * 0.02
        B = jax.random.normal(kb, (N_ADAPTERS, RANK, IN_F), dtype=jnp.float32) * 0.02
        adapter_ids = jax.random.randint(ki, (BATCH,), 0, N_ADAPTERS, dtype=jnp.int32)
        return {'x': x, 'A': A, 'B': B, 'adapter_ids': adapter_ids}
    _L3_cond_all = _L3_cond_setup()
    _L3_cond_in = {k: v for k, v in _L3_cond_all.items() if k in ('A', 'B')}
    del _L3_cond_all
    return {'x': x, 'itok_Bx16_0_63': itok_Bx16_0_63, 'itok_B_207_1644': itok_B_207_1644, 'itok_B_0_15': itok_B_0_15, 'condB_scale': condB_scale, 'itok_Bx4096x4096_0_255': itok_Bx4096x4096_0_255, 'condB_wscale': condB_wscale, 'itok_Bx4096_0_255': itok_Bx4096_0_255, 'condB_bscale': condB_bscale, 'itok_B_3_7': itok_B_3_7, '_lenS': _lenS, 'L0_cond_Wq': _L0_cond_in['Wq'], 'L0_cond_Wk': _L0_cond_in['Wk'], 'L0_cond_Wv': _L0_cond_in['Wv'], 'L0_cond_Wo': _L0_cond_in['Wo'], 'L0_cond_q_norm_w': _L0_cond_in['q_norm_w'], 'L0_cond_k_norm_w': _L0_cond_in['k_norm_w'], 'L0_cond_k_cache': _L0_cond_in['k_cache'], 'L0_cond_v_cache': _L0_cond_in['v_cache'], 'L1_cond_weights': _L1_cond_in['weights'], 'L2_cond_weight': _L2_cond_in['weight'], 'L2_cond_bias': _L2_cond_in['bias'], 'L3_cond_A': _L3_cond_in['A'], 'L3_cond_B': _L3_cond_in['B']}

def reference(x, itok_Bx16_0_63, itok_B_207_1644, itok_B_0_15, condB_scale, itok_Bx4096x4096_0_255, condB_wscale, itok_Bx4096_0_255, condB_bscale, itok_B_3_7, _lenS, L0_cond_Wq, L0_cond_Wk, L0_cond_Wv, L0_cond_Wo, L0_cond_q_norm_w, L0_cond_k_norm_w, L0_cond_k_cache, L0_cond_v_cache, L1_cond_weights, L2_cond_weight, L2_cond_bias, L3_cond_A, L3_cond_B):
    import jax
    import jax.numpy as jnp

    def _L0_cond_ref(x, Wq, Wk, Wv, Wo, q_norm_w, k_norm_w, k_cache, v_cache, block_table, cache_seqlens):
        import jax, jax.numpy as jnp
        import numpy as np
        B, S, HID = (4, 128, 512)
        D, HQ, HK = (128, 32, 8)
        PAGES, PSIZE, NPP = (64, 32, 16)
        THETA = 10000.0
        EPS = 1e-06
        SCALE = 1.0 / float(np.sqrt(D))

        def _rmsnorm(t, w):
            var = jnp.mean(t * t, axis=-1, keepdims=True)
            return t * jax.lax.rsqrt(var + EPS) * w

        def _rope(t, pos):
            inv_freq = 1.0 / THETA ** (jnp.arange(0, D, 2, dtype=jnp.float32) / D)
            freqs = pos[..., None].astype(jnp.float32) * inv_freq
            cos = jnp.cos(freqs)[:, :, None, :]
            sin = jnp.sin(freqs)[:, :, None, :]
            t1, t2 = (t[..., :D // 2], t[..., D // 2:])
            return jnp.concatenate([t1 * cos - t2 * sin, t2 * cos + t1 * sin], axis=-1)
        bsz, seqlen, _ = x.shape
        q = jnp.einsum('bsd,ed->bse', x, Wq).reshape(bsz, seqlen, HQ, D)
        k = jnp.einsum('bsd,ed->bse', x, Wk).reshape(bsz, seqlen, HK, D)
        v = jnp.einsum('bsd,ed->bse', x, Wv).reshape(bsz, seqlen, HK, D)
        q = _rmsnorm(q, q_norm_w)
        k = _rmsnorm(k, k_norm_w)
        pos = cache_seqlens[:, None] + jnp.arange(seqlen)[None, :]
        q = _rope(q, pos)
        k = _rope(k, pos)
        L = NPP * PSIZE
        kc = k_cache[block_table].reshape(bsz, L, HK, D)
        vc = v_cache[block_table].reshape(bsz, L, HK, D)
        k_all = jnp.concatenate([kc, k], axis=1)
        v_all = jnp.concatenate([vc, v], axis=1)
        valid_c = jnp.arange(L)[None, :] < cache_seqlens[:, None]
        valid = jnp.concatenate([valid_c, jnp.ones((bsz, seqlen), dtype=bool)], axis=1)
        rep = HQ // HK
        k_all = jnp.repeat(k_all, rep, axis=2)
        v_all = jnp.repeat(v_all, rep, axis=2)
        scores = jnp.einsum('bqhd,bkhd->bhqk', q, k_all) * SCALE
        scores = jnp.where(valid[:, None, None, :], scores, -1e+30)
        probs = jax.nn.softmax(scores, axis=-1)
        o = jnp.einsum('bhqk,bkhd->bqhd', probs, v_all)
        o = o.reshape(bsz, seqlen, HQ * D)
        return jnp.einsum('bse,de->bsd', o, Wo)

    def _L1_cond_ref(x, weights, condition):
        import jax, jax.numpy as jnp
        import numpy as np
        NUM_CONDITIONS = 16
        IN_CH = 32
        OUT_CH = 32
        B = 64
        T = 512
        W = weights[condition]
        return jnp.einsum('bct,bcd->bdt', x, W)

    def _L2_cond_ref(x, weight, bias, scale, wq, wscale, wzp, bq, bscale, bzp):
        import jax, jax.numpy as jnp
        import numpy as np
        f32 = jnp.float32
        dW = jnp.einsum('i,ijk->jk', scale * wscale, wq.astype(f32)) + jnp.dot(scale, wzp.astype(f32))
        W = weight + dW
        db = jnp.einsum('i,ij->j', scale * bscale, bq.astype(f32)) + jnp.dot(scale, bzp.astype(f32))
        b = bias + db
        return jnp.einsum('bsi,oi->bso', x, W) + b

    def _L3_cond_ref(x, A, B, adapter_ids):
        import jax, jax.numpy as jnp
        import numpy as np
        RANK = 16
        ALPHA = 16.0
        SCALING = ALPHA / RANK
        N_ADAPTERS = 8
        IN_F = 512
        OUT_F = 512
        BATCH = 4
        SEQ = 256
        B_sel = B[adapter_ids]
        A_sel = A[adapter_ids]
        Bx = jnp.einsum('bni,bri->bnr', x, B_sel)
        out = jnp.einsum('bnr,bor->bno', Bx, A_sel)
        return out * SCALING
    x = x + _L0_cond_ref(x, L0_cond_Wq, L0_cond_Wk, L0_cond_Wv, L0_cond_Wo, L0_cond_q_norm_w, L0_cond_k_norm_w, L0_cond_k_cache, L0_cond_v_cache, itok_Bx16_0_63, itok_B_207_1644)
    x = x + _L1_cond_ref(x, L1_cond_weights, itok_B_0_15)
    x = x + _L2_cond_ref(x, L2_cond_weight, L2_cond_bias, condB_scale, itok_Bx4096x4096_0_255, condB_wscale, _lenS, itok_Bx4096_0_255, condB_bscale, _lenS)
    x = x + _L3_cond_ref(x, L3_cond_A, L3_cond_B, itok_B_3_7)
    return x

_drawn_inputs = setup_inputs


def setup_inputs(seed=0):
    import zlib

    import numpy as np

    out = dict(_drawn_inputs(seed))
    spreads = {}
    factors = {'condB_wscale': 64.0,
     'condB_bscale': 200.0,
     'L0_cond_Wk': 8.0,
     'L0_cond_Wv': 8.0,
     'L0_cond_k_norm_w': 8.0,
     'L2_cond_weight': 3.218,
     'L2_cond_bias': 200.0,
     'L0_cond_k_cache': 4.559,
     'L0_cond_v_cache': 2.984}
    for name, (base, spread) in spreads.items():
        noise = np.random.default_rng([zlib.crc32(name.encode()), seed]).standard_normal(out[name].shape)
        drawn = base * np.exp(spread * noise) if base else spread * noise
        out[name] = jnp.asarray(drawn.astype(out[name].dtype))
    for name, factor in factors.items():
        out[name] = (out[name] * factor).astype(out[name].dtype)
    return out
```

```python
import numpy as np
import concourse.bass as bass
from concourse import mybir
from contextlib import ExitStack

F32 = mybir.dt.float32
I32 = mybir.dt.int32
BF16 = mybir.dt.bfloat16
ALU = mybir.AluOpType
ACT = mybir.ActivationFunctionType
AX = mybir.AxisListType

B, S, HID = 32, 32, 512
D, HQ, HK = 128, 32, 8
REP = HQ // HK
PAGES, PSIZE, NPP = 64, 32, 16
L = NPP * PSIZE
KEYS = L + S
P = 128
KC = HID // P
BT = P // S
TILES = B // BT
GH = 2
GROUPS = HK // GH
QH = GH * REP
ROUNDS = GROUPS * TILES
PAIRS = BT * GH
HALF = PAIRS // 2
CH = L // P
PCOLS = (CH + 1) * P
QKV = (QH + 2 * GH) * D
NORMED = QH + GH
CONDS, NAD, RANK = 16, 8, 16
SCALE = 1.0 / float(np.sqrt(D))
EPS = 1e-6
MASKED = -1e30
TWO_PI = 2.0 * np.pi
PI_1 = 6.28125
PI_2 = float(np.float32(np.round((TWO_PI - PI_1) * 2.0 ** 22) / 2.0 ** 22))
PI_3 = float(TWO_PI - PI_1 - PI_2)
ROUNDER = 1.5 * 2.0 ** 23
PI_F = 3.1415925


def constants():
    key_pos = np.concatenate([np.arange(L), np.full(S, -2.0 ** 31)]).astype(np.float32)
    inv_freq = (1.0 / np.float32(10000.0) ** (np.arange(0, D, 2, dtype=np.float32) / np.float32(D))).astype(np.float32)
    lane = np.arange(P)
    cols = np.zeros((P, 8), np.float32)
    cols[:, 0] = lane % S
    cols[:, 1] = lane // RANK
    cols[:, 2] = -0.5
    return {
        "c_ident": np.eye(P, dtype=np.float32),
        "c_key_pos": np.broadcast_to(key_pos, (P, KEYS)).copy(),
        "c_inv_freq": np.broadcast_to(inv_freq, (P, D // 2)).copy(),
        "c_cols": cols,
    }


def build(nc, t):
    ctx = ExitStack()
    with ctx:
        def sb(name, shape, dt=F32):
            return ctx.enter_context(nc.sbuf_tensor(name + "_sb", shape, dt))

        def sem(name):
            return ctx.enter_context(nc.semaphore(name))

        ident = sb("ident", [P, P])
        key_pos = sb("key_pos", [P, KEYS])
        cols = sb("cols", [P, 8])
        acc = sb("acc", [P, TILES, HID])
        wqkv = sb("wqkv", [P, KC, QKV])
        wo = sb("wo", [P, QH, HID])
        xT = sb("xT", [P, KC, P])
        qraw = sb("qraw", [P, NORMED, D])
        rope_a = sb("rope_a", [P, NORMED, D])
        rope_b = sb("rope_b", [P, NORMED, D])
        qrope = sb("qrope", [P, NORMED, D])
        ssq = sb("ssq", [P, NORMED])
        squared = sb("squared", [P, NORMED, D])
        rstd = sb("rstd", [P, NORMED])
        varr = sb("varr", [P, NORMED])
        v_nat = sb("v_nat", [P, GH * D])
        v_new = sb("v_new", [P, BT, GH * D])
        qT = sb("qT", [P, GH, BT, REP * S])
        kT_new = sb("kT_new", [P, GH, P])
        kv = sb("kv", [P, BT, CH, 2 * GH * D])
        kT = sb("kT", [P, 2, L])
        sc = sb("sc", [P, 2, KEYS])
        bias = sb("bias", [P, 2])
        probs = sb("probs", [P, 2, PCOLS])
        sums = sb("sums", [P, PAIRS])
        inv = sb("inv", [P, PAIRS])
        pT = sb("pT", [P, 2, PCOLS])
        o_nat = sb("o_nat", [P, HALF, D])
        oT = sb("oT", [P, QH, BT, S])
        page_rows = sb("page_rows", [P, GROUPS, B * CH], I32)
        rows_now = sb("rows_now", [P, BT, CH], I32)
        lens = sb("lens", [P, B])
        mask = sb("mask", [P, BT, KEYS], BF16)
        rope_c = sb("rope_c", [P, TILES, 2, D])
        rope_s = sb("rope_s", [P, TILES, 2, D])
        wT = sb("wT", [P, KC, HID])
        wq_in = sb("wq_in", [P, KC * HID], I32)
        dscale = sb("dscale", [P, B])
        small = sb("small", [P, 8, B])
        bias_row = sb("bias_row", [P, HID])

        psum = ctx.enter_context(nc.psum_tensor("psum", [P, 8 * 512], F32))

        def bank(b, n=512):
            return psum[:, 512 * b:512 * b + n]

        SC, PT, KT, O, MA, MB = 0, 2, 4, 5, 6, 7

        names = """consts_in params_in tabs_in xt_in w_in wo_in vnew_in wq_loaded
            pool_waits vector_waits sync_waits kv_in0 kv_in1 kv_in2 kv_in3 kv_used0 kv_used1 kv_used2 kv_used3 zeroed rows_now_in0 rows_now_in1 rows_now_in2 rows_now_in3 mix_in rows_v angles
            kt_psum kt_sb s_psum s_done p_sb pt_psum pt_sb pv_done o_sb ot_psum ot_sb
            qt_psum qt_sb_a qt_sb_v kn_psum kn_sb proj_psum raw_a raw_v v_sb
            sq_done ssq_done rstd_done ab_done roped rope_add mask_done lens_now_in var_done
            wo_psum acc_done dw_now dw_done chain pchain achain tables
            bq_psum cond_in l1_in bd_done f_cp f_x2p f_x2s f_x3p f_x3s f_x3tp f_x3ts f_bxp f_bxs f_yp f_out out_dma bias_done wdone tail_p""".split()
        s = {n: sem(n) for n in names}

        x1_now = qraw[:, 0:4, :].rearrange("p h d -> p (h d)")
        x2T = qraw[:, 4:8, :]
        x3 = rope_a[:, 0:4, :].rearrange("p h d -> p (h d)")
        x3T = rope_a[:, 4:8, :]
        y = rope_b[:, 0:4, :].rearrange("p h d -> p (h d)")
        bx = rope_b[:, 4, :]
        mix = rope_b[:, 6, :]
        bT = wqkv[:, 0, 0:KC * P].rearrange("p (k r) -> p k r", k=KC)
        aT = wqkv[:, 1, 0:HID]
        adapter = wqkv[:, 2, 0:B * S]
        bq_i = wqkv[0:B, 3, 0:HID].bitcast(I32)
        bq_f = wqkv[0:B, 3, HID:2 * HID]
        wb = wqkv[0:B, 3, 2 * HID:2 * HID + P]
        bcol = sb("bcol", [P, 8])
        mix_all = sb("mix_all", [P, TILES, S])
        cond_i = sb("cond_i", [P, TILES], I32)
        mix_rows = sb("mix_rows", [P, TILES], I32)
        aid_i = sb("aid_i", [P, B * S], I32)

        block = ctx.enter_context(nc.Block())

        @block.sync
        def _(sp):
            sp.dma_start(ident[:], t["c_ident"]).then_inc(s["consts_in"], 16)
            sp.dma_start(key_pos[:], t["c_key_pos"]).then_inc(s["consts_in"], 16)
            sp.dma_start(cols[:], t["c_cols"]).then_inc(s["consts_in"], 16)
            sp.dma_start(kT[:, 0, 0:B * CH].bitcast(I32), t["tbl_rep"]).then_inc(s["params_in"], 16)
            sp.dma_start(small[:, 0, :].bitcast(I32), t["len_rep"]).then_inc(s["params_in"], 16)
            sp.dma_start(small[:, 1, 0:TILES].bitcast(I32), t["pos_rep"]).then_inc(s["params_in"], 16)
            sp.dma_start(cond_i[:], t["cond_rep"]).then_inc(s["params_in"], 16)
            sp.dma_start(small[:, 2, :], t["scale_rep"]).then_inc(s["params_in"], 16)
            sp.dma_start(small[:, 3, :], t["wscale_rep"]).then_inc(s["params_in"], 16)
            sp.dma_start(small[:, 4, :].bitcast(I32), t["zp_rep"]).then_inc(s["params_in"], 16)
            sp.dma_start(rope_a[:, 0, 0:D // 2], t["c_inv_freq"]).then_inc(s["params_in"], 16)
            sp.dma_start(rope_a[:, 1, :], t["q_norm_rep"]).then_inc(s["params_in"], 16)
            sp.dma_start(rope_a[:, 2, :], t["k_norm_rep"]).then_inc(s["params_in"], 16)
            sp.dma_start(acc[:], t["x_nat"]).then_inc(s["params_in"], 16)
            sp.dma_start(wT[:], t["weightT"]).then_inc(s["params_in"], 16)
            sp.dma_start(bias_row[:], t["bias_rep"]).then_inc(s["params_in"], 16)
            sp.wait_ge(s["tables"], 1)

            def load_round(m, i):
                sp.wait_ge(s["proj_psum"], m * 3)
                sp.sem_inc(s["sync_waits"], 1)
                sp.dma_start(xT[:], t["xT"][bass.ds(i, 1)].rearrange("a p k n -> p (a k) n")).then_inc(s["xt_in"], 16)
                sp.wait_ge(s["dw_done"], m)
                sp.sem_inc(s["sync_waits"], 1)
                sp.dma_start(wq_in[:], t["wq"][bass.ds(m, 1)].rearrange("a p n -> (a p) n")).then_inc(s["wq_loaded"], 16)
                sp.wait_ge(s["v_sb"], m + 1)
                sp.sem_inc(s["sync_waits"], 1)
                sp.wait_ge(s["pv_done"], m * PAIRS)
                sp.sem_inc(s["sync_waits"], 1)
                for b in range(BT):
                    sp.dma_start(v_new[0:S, b, :], v_nat[S * b:S * (b + 1), :]).then_inc(s["vnew_in"], 16)

            with sp.Fori(0, GROUPS) as g:
                sp.wait_ge(s["proj_psum"], g * (3 * TILES))
                sp.sem_inc(s["sync_waits"], 1)
                sp.dma_start(wqkv[:], t["wqkv"][bass.ds(g, 1)].rearrange("a p k n -> p (a k) n")).then_inc(s["w_in"], 16)
                sp.wait_ge(s["w_in"], (g + 1) * 16)
                sp.sem_inc(s["sync_waits"], 1)
                load_round(g * TILES, 0)
                sp.wait_ge(s["wo_psum"], g * TILES)
                sp.sem_inc(s["sync_waits"], 1)
                sp.dma_start(wo[:], t["wo"][bass.ds(g, 1)].rearrange("a p h n -> p (a h) n")).then_inc(s["wo_in"], 16)
                sp.wait_ge(s["wo_in"], (g + 1) * 16)
                sp.sem_inc(s["sync_waits"], 1)
                with sp.Fori(1, TILES) as i:
                    load_round(g * TILES + i, i)
            sp.wait_ge(s["proj_psum"], 3 * ROUNDS)
            sp.dma_start(bT, t["B_all"]).then_inc(s["tabs_in"], 16)
            sp.dma_start(aT, t["A_all"]).then_inc(s["tabs_in"], 16)
            sp.dma_start(aid_i[:], t["aid_rep"]).then_inc(s["tabs_in"], 16)
            sp.dma_start(bq_i, t["bq"]).then_inc(s["tabs_in"], 16)
            sp.dma_start(bcol[0:B, 0:1], t["scale_col"]).then_inc(s["tabs_in"], 16)
            sp.dma_start(bcol[0:B, 1:2], t["bscale_col"]).then_inc(s["tabs_in"], 16)
            with sp.Fori(0, TILES) as i:
                sp.wait_ge(s["f_out"], i + 1)
                sp.sem_inc(s["sync_waits"], 1)
                sp.dma_start(t["out"][bass.ds(i, 1)].rearrange("a p n -> (a p) n"), y).then_inc(s["out_dma"], 16)
            sp.wait_ge(s["out_dma"], 16 * TILES)

        @block.gpsimd
        def _(po):
            po.memset(probs[:], 0.0).then_inc(s["zeroed"], 1)
            po.memset(v_new[:], 0.0).then_inc(s["zeroed"], 1)
            po.wait_ge(s["tables"], 1)
            rows = page_rows[:].rearrange("p g c -> p (g c)")

            def inverse_root(m1):
                po.wait_ge(s["ssq_done"], m1)
                po.sem_inc(s["pool_waits"], 1)
                po.tensor_scalar(varr[:], ssq[:], 1.0 / D, EPS, ALU.mult, ALU.add).then_inc(s["var_done"], 1)
                po.wait_ge(s["var_done"], m1)
                po.sem_inc(s["pool_waits"], 1)
                po.tensor_tensor(rstd[:], varr[:], cols[:, 2:3].to_broadcast([P, NORMED]), ALU.pow).then_inc(s["rstd_done"], 1)

            for i in range(TILES):
                po.indirect_dma_start(out=mix_all[:, i, :], out_offset=None, in_=t["mix"],
                                      in_offset=bass.IndirectOffsetOnAxis(ap=mix_rows[:, i:i + 1], axis=0)
                                      ).then_inc(s["mix_in"], 16)
            inverse_root(1)

            def round_(n, last):
                for b in range(BT):
                    po.wait_ge(s[f"kv_used{b}"], n - 1)
                    po.sem_inc(s["pool_waits"], 1)
                    po.tensor_copy(rows_now[:, b, :], rows[:, bass.ds((n - 1) * (BT * CH) + b * CH, CH)]
                                   ).then_inc(s[f"rows_now_in{b}"], 1)
                    po.wait_ge(s[f"rows_now_in{b}"], n)
                    po.sem_inc(s["pool_waits"], 1)
                    for c in range(CH):
                        po.indirect_dma_start(out=kv[:, b, c, :], out_offset=None, in_=t["kv"],
                                              in_offset=bass.IndirectOffsetOnAxis(ap=rows_now[:, b, c:c + 1], axis=0)
                                              ).then_inc(s[f"kv_in{b}"], 16)
                if not last:
                    inverse_root(n + 1)

            with po.Fori(1, ROUNDS) as n:
                round_(n, False)
            round_(ROUNDS, True)

        @block.scalar
        def _(act):
            sin_t = qrope[:, 0:4, :].rearrange("p h d -> p (h d)")
            cos_t = qrope[:, 4:8, :].rearrange("p h d -> p (h d)")
            act.wait_ge(s["angles"], 1)
            nc.scalar.activation(sin_t, sin_t, ACT.Sin)
            nc.scalar.activation(cos_t, cos_t, ACT.Sin).then_inc(s["achain"], 1)

            def take_proj(m, first=False):
                act.wait_ge(s["proj_psum"], 3 * m + 1)
                if not first:
                    act.wait_ge(s["roped"], m)
                else:
                    act.wait_ge(s["tables"], 1)
                nc.scalar.copy(qraw[:, 0:REP, :].rearrange("p h d -> p (h d)"), bank(MA)).then_inc(s["raw_a"], 1)

            def take_kv(m, first=False):
                act.wait_ge(s["proj_psum"], 3 * m + 3)
                nc.scalar.copy(qraw[:, QH:NORMED, :].rearrange("p h d -> p (h d)"), bank(MA, GH * D)).then_inc(s["raw_a"], 1)
                if not first:
                    act.wait_ge(s["vnew_in"], m * (16 * BT))
                nc.scalar.copy(v_nat[:], psum[:, 512 * MA + GH * D:512 * (MA + 1)]).then_inc(s["v_sb"], 1)

            def squares(m):
                act.wait_ge(s["raw_v"], m + 1)
                act.wait_ge(s["raw_a"], 2 * m + 2)
                act.wait_ge(s["rstd_done"], m)
                for h in range(NORMED):
                    ins = nc.scalar.activation(squared[:, h, :], qraw[:, h, :], ACT.Square, accum_out=ssq[:, h:h + 1])
                ins.then_inc(s["ssq_done"], 1)

            def take_queries(n):
                act.wait_ge(s["qt_psum"], 2 * n + 1)
                nc.scalar.copy(qT[:, 0].rearrange("p b (j s) -> p j b s", j=REP),
                               bank(MA).rearrange("p (j b s) -> p j b s", j=REP, b=BT)).then_inc(s["qt_sb_a"], 1)
                act.wait_ge(s["kn_psum"], n + 1)
                nc.scalar.copy(kT_new[:].rearrange("p h k -> p (h k)"), bank(MA, GH * P)).then_inc(s["kn_sb"], 1)

            def keys(n, i):
                act.wait_ge(s["kt_psum"], n * PAIRS + (i + 1))
                nc.scalar.copy(kT[:, i % 2, :], bank(KT)).then_inc(s["kt_sb"], 1)

            take_proj(0, True)
            take_kv(0, True)
            squares(0)
            take_queries(0)
            keys(0, 0)

            def round_(n, last):
                for i in range(PAIRS + 2):
                    if i + 1 < PAIRS:
                        keys(n, i + 1)
                    if i < PAIRS:
                        act.wait_ge(s["s_done"], n * PAIRS + (i + 1))
                        act.wait_ge(s["pt_psum"], n * PAIRS + (i - 1 if i >= 2 else 0))
                        nc.scalar.activation(probs[:, i % 2, 0:KEYS], sc[:, i % 2, :], ACT.Exp, bias=bias[:, i % 2:i % 2 + 1],
                                             scale=-1.0, accum_out=sums[:, i:i + 1]).then_inc(s["p_sb"], 1)
                    if i == 0 and not last:
                        take_proj(n + 1)
                    if i == 2 and not last:
                        take_kv(n + 1)
                    if i == 3 and not last:
                        squares(n + 1)
                    if i == 6:
                        take_outputs(n, 0)
                if not last:
                    take_queries(n + 1)
                    keys(n + 1, 0)
                take_outputs(n, 1)

            def take_outputs(n, half):
                act.wait_ge(s["ot_psum"], 2 * n + (half + 1))
                nb = BT // 2
                nc.scalar.copy(oT[:, :, nb * half:nb * (half + 1), :].rearrange("p h b s -> p b h s"),
                               bank(MB).rearrange("p (b h s) -> p b h s", b=nb, h=QH)).then_inc(s["ot_sb"], 1)

            with act.Fori(0, ROUNDS - 1) as n:
                round_(n, False)
            round_(ROUNDS - 1, True)

            with act.Fori(0, TILES) as i:
                act.wait_ge(s["f_x2p"], i + 1)
                nc.scalar.copy(x2T.rearrange("p k n -> p (k n)"), bank(0)).then_inc(s["f_x2s"], 1)
                act.wait_ge(s["f_x3tp"], i + 1)
                nc.scalar.copy(x3T.rearrange("p k n -> p (k n)"), bank(2)).then_inc(s["f_x3ts"], 1)

        @block.vector
        def _(v):
            link = [0]

            def chained(ins):
                link[0] += 1
                ins.then_inc(s["chain"], 1)
                v.wait_ge(s["chain"], link[0])

            v.wait_ge(s["consts_in"], 16 * 3)
            v.wait_ge(s["params_in"], 16 * 13)
            tbl = kT[:, 0, 0:B * CH].bitcast(I32)
            row_f = kT[:, 1, 0:B * CH]
            chained(nc.vector.tensor_scalar(row_f, tbl, float(PSIZE), cols[:, 0:1], ALU.mult, ALU.add))
            for g in range(GROUPS):
                chained(nc.vector.tensor_scalar(page_rows[:, g, :], row_f, float(g * PAGES * PSIZE), None, ALU.add))
            chained(nc.vector.tensor_copy(lens[:], small[:, 0, :].bitcast(I32)))
            pos_i = small[:, 1, 0:TILES].bitcast(I32)
            chained(nc.vector.tensor_copy(small[:, 5, 0:TILES], pos_i))
            chained(nc.vector.tensor_scalar(small[:, 6, 0:TILES], small[:, 5, 0:TILES], cols[:, 0:1], None, ALU.add))
            HD = D // 2
            ang = rope_b[:, 0:4, :].rearrange("p h d -> p (h d)")
            turns = rope_b[:, 4:8, :].rearrange("p h d -> p (h d)")
            for i in range(TILES):
                chained(nc.vector.tensor_scalar(ang[:, HD * i:HD * (i + 1)], rope_a[:, 0, 0:HD], small[:, 6, i:i + 1], None, ALU.mult))
            for quarter, dst in ((0.0, qrope[:, 0:4, :]), (0.25, qrope[:, 4:8, :])):
                r = dst.rearrange("p h d -> p (h d)")
                chained(nc.vector.tensor_scalar(turns, ang, 1.0 / TWO_PI, quarter, ALU.mult, ALU.add))
                chained(nc.vector.tensor_scalar(turns, turns, ROUNDER, None, ALU.add))
                chained(nc.vector.tensor_scalar(turns, turns, -ROUNDER, None, ALU.add))
                chained(nc.vector.scalar_tensor_tensor(r, turns, -PI_1, ang, ALU.mult, ALU.add))
                chained(nc.vector.scalar_tensor_tensor(r, turns, -PI_2, r, ALU.mult, ALU.add))
                chained(nc.vector.scalar_tensor_tensor(r, turns, -PI_3, r, ALU.mult, ALU.add))
                if quarter:
                    chained(nc.vector.tensor_scalar(r, r, TWO_PI / 4, None, ALU.add))
                ins = nc.vector.tensor_scalar(r, r, PI_F, -PI_F, ALU.min, ALU.max)
                if not quarter:
                    chained(ins)
            ins.then_inc(s["angles"], 1)
            v.wait_ge(s["achain"], 1)
            sin_t = qrope[:, 0:4, :].rearrange("p h d -> p (h d)").rearrange("p (t d) -> p t d", t=TILES)
            cos_t = qrope[:, 4:8, :].rearrange("p h d -> p (h d)").rearrange("p (t d) -> p t d", t=TILES)
            for kind in range(2):
                w1 = rope_a[:, 1 + kind, 0:HD].unsqueeze(1).to_broadcast([P, TILES, HD])
                w2 = rope_a[:, 1 + kind, HD:D].unsqueeze(1).to_broadcast([P, TILES, HD])
                chained(nc.vector.tensor_tensor(rope_c[:, :, kind, 0:HD], cos_t, w1, ALU.mult))
                chained(nc.vector.tensor_tensor(rope_c[:, :, kind, HD:D], cos_t, w2, ALU.mult))
                chained(nc.vector.scalar_tensor_tensor(rope_s[:, :, kind, 0:HD], sin_t, -1.0, w2, ALU.mult, ALU.mult))
                chained(nc.vector.tensor_tensor(rope_s[:, :, kind, HD:D], sin_t, w1, ALU.mult))
            chained(nc.vector.tensor_tensor(dscale[:], small[:, 2, :], small[:, 3, :], ALU.mult))
            chained(nc.vector.tensor_copy(small[:, 5, :], small[:, 4, :].bitcast(I32)))
            chained(nc.vector.tensor_tensor(small[:, 6, :], small[:, 5, :], small[:, 2, :], ALU.mult))
            chained(nc.vector.tensor_reduce(small[:, 7, 0:1], small[:, 6, :], AX.X, ALU.add))
            chained(nc.vector.tensor_scalar(wT[:], wT[:], small[:, 7, 0:1], None, ALU.add))
            chained(nc.vector.tensor_scalar(bias_row[:], bias_row[:], small[:, 7, 0:1], None, ALU.add))
            chained(nc.vector.tensor_copy(small[:, 5, 0:TILES], cond_i[:]))
            chained(nc.vector.tensor_scalar(mix_rows[:], small[:, 5, 0:TILES], float(S), cols[:, 0:1], ALU.mult, ALU.add))
            v.wait_ge(s["zeroed"], 2)
            v.memset(small[:, 0, 0:1], 0.0).then_inc(s["tables"], 1)

            def take_proj(m, first=False):
                v.wait_ge(s["proj_psum"], 3 * m + 2)
                if not first:
                    v.wait_ge(s["roped"], m)
                nc.vector.tensor_copy(qraw[:, REP:QH, :].rearrange("p h d -> p (h d)"), bank(MB)).then_inc(s["raw_v"], 1)

            def rotate(m, tile):
                v.wait_ge(s["raw_a"], 2 * m + 2)
                v.wait_ge(s["raw_v"], m + 1)
                v.wait_ge(s["ab_done"], m)
                for kind, lo, hi in ((0, 0, QH), (1, QH, NORMED)):
                    n_h = hi - lo
                    c = rope_c[:, tile, kind, :].rearrange("p a d -> p (a d)").unsqueeze(1).to_broadcast([P, n_h, D])
                    nc.vector.tensor_tensor(rope_a[:, lo:hi, :], qraw[:, lo:hi, :], c, ALU.mult)
                    for half in range(2):
                        other = 1 - half
                        sn = rope_s[:, tile, kind, HD * half:HD * (half + 1)].rearrange("p a d -> p (a d)").unsqueeze(1).to_broadcast([P, n_h, HD])
                        ins = nc.vector.tensor_tensor(rope_b[:, lo:hi, HD * half:HD * (half + 1)],
                                                      qraw[:, lo:hi, HD * other:HD * (other + 1)], sn, ALU.mult)
                ins.then_inc(s["roped"], 1)

            def add_halves(m):
                v.wait_ge(s["roped"], m + 1)
                nc.vector.tensor_tensor(rope_a[:], rope_a[:], rope_b[:], ALU.add).then_inc(s["rope_add"], 1)

            def normalise(m):
                v.wait_ge(s["rstd_done"], m + 1)
                v.wait_ge(s["rope_add"], m + 1)
                v.wait_ge(s["kn_psum"], m)
                nc.vector.tensor_tensor(qrope[:], rope_a[:], rstd[:].unsqueeze(2).to_broadcast([P, NORMED, D]),
                                        ALU.mult).then_inc(s["ab_done"], 1)

            def take_queries(n):
                v.wait_ge(s["qt_psum"], 2 * n + 2)
                nc.vector.tensor_copy(qT[:, 1].rearrange("p b (j s) -> p j b s", j=REP),
                                      bank(MB).rearrange("p (j b s) -> p j b s", j=REP, b=BT)).then_inc(s["qt_sb_v"], 1)

            def set_mask(b, batch):
                nc.vector.tensor_scalar(mask[:, b, :], key_pos[:], lens[:, batch], MASKED, ALU.is_ge, ALU.mult).then_inc(s["mask_done"], 1)

            take_proj(0, True)
            for b in range(BT):
                set_mask(b, slice(b, b + 1))
            rotate(0, slice(0, 1))
            add_halves(0)
            normalise(0)
            take_queries(0)

            def round_(n, next_tile, last):
                for i in range(PAIRS + 2):
                    if i < PAIRS:
                        if i % GH == 0:
                            v.wait_ge(s["mask_done"], n * BT + (i // GH + 1))
                        if i >= 2:
                            v.wait_ge(s["p_sb"], n * PAIRS + (i - 1))
                        else:
                            v.wait_ge(s["p_sb"], n * PAIRS)
                        v.wait_ge(s["s_psum"], n * PAIRS + (i + 1))
                        v.sem_inc(s["vector_waits"], 1)
                        nc.vector.tensor_tensor_reduce(out=sc[:, i % 2, :], in0=psum[:, 512 * SC:512 * SC + KEYS],
                                                       in1=mask[:, i // GH, :], scale=-SCALE, scalar=3e38,
                                                       op0=ALU.add, op1=ALU.min,
                                                       accum_out=bias[:, i % 2:i % 2 + 1]).then_inc(s["s_done"], 1)
                    if 1 <= i <= PAIRS:
                        j = i - 1
                        if j >= 2:
                            v.wait_ge(s["pv_done"], n * PAIRS + (j - 1))
                        else:
                            v.wait_ge(s["pv_done"], n * PAIRS)
                        v.wait_ge(s["pt_psum"], n * PAIRS + (j + 1))
                        nc.vector.tensor_copy(pT[:, j % 2, :], psum[:, 512 * PT:512 * PT + PCOLS]).then_inc(s["pt_sb"], 1)
                    if not last and i >= 2 and i % GH == 0:
                        b = i // GH - 1
                        set_mask(b, bass.ds((n + 1) % TILES * BT + b, 1))
                    if i == 0:
                        v.wait_ge(s["dw_done"], n)
                        v.wait_ge(s["wq_loaded"], 16 * (n + 1))
                        wflat = wT[:].rearrange("p k n -> p (k n)")
                        nc.vector.scalar_tensor_tensor(wflat, wq_in[:], dscale[:, bass.ds(n, 1)] if not last else dscale[:, n:n + 1], wflat, ALU.mult, ALU.add).then_inc(s["dw_done"], 1)
                    if i == 2 and not last:
                        take_proj(n + 1)
                    if i == 3 and not last:
                        rotate(n + 1, next_tile)
                    if i == 4 and not last:
                        add_halves(n + 1)
                    if i == 5:
                        outputs(n, 0)
                    if i == 6 and not last:
                        normalise(n + 1)
                outputs(n, 1)
                if not last:
                    take_queries(n + 1)
                v.wait_ge(s["wo_psum"], n + 1)
                tile = bass.ds(n % TILES, 1) if last is not True else slice(TILES - 1, TILES)
                a = acc[:, tile, :].rearrange("p a n -> p (a n)")
                nc.vector.tensor_tensor(a, bank(MA), a, ALU.add).then_inc(s["acc_done"], 1)

            def outputs(n, half):
                v.wait_ge(s["p_sb"], n * PAIRS + HALF * (half + 1))
                nc.vector.reciprocal(inv[:, HALF * half:HALF * (half + 1)], sums[:, HALF * half:HALF * (half + 1)]).then_inc(s["rows_v"], 1)
                v.wait_ge(s["rows_v"], 2 * n + (half + 1))
                v.wait_ge(s["pv_done"], n * PAIRS + HALF * (half + 1))
                nc.vector.tensor_tensor(o_nat[:], bank(O).rearrange("p (i d) -> p i d", i=HALF),
                                        inv[:, HALF * half:HALF * (half + 1)].unsqueeze(2).to_broadcast([P, HALF, D]),
                                        ALU.mult).then_inc(s["o_sb"], 1)

            with v.Fori(0, ROUNDS - 1) as n:
                round_(n, bass.ds((n + 1) % TILES, 1), False)
            round_(ROUNDS - 1, None, True)

            link[0] = 0

            def tail(ins):
                link[0] += 1
                ins.then_inc(s["tail_p"], 1)
                v.wait_ge(s["tail_p"], link[0])

            v.wait_ge(s["tabs_in"], 16 * 6)
            tail(nc.vector.tensor_copy(adapter, aid_i[:]))
            tail(nc.vector.tensor_scalar(adapter, adapter, cols[:, 1:2], None, ALU.is_equal))
            tail(nc.vector.tensor_copy(bq_f, bq_i))
            tail(nc.vector.tensor_tensor(bcol[0:B, 3:4], bcol[0:B, 0:1], bcol[0:B, 1:2], ALU.mult))
            nc.vector.tensor_copy(wb, bcol[0:B, 3:4].to_broadcast([B, P])).then_inc(s["wdone"], 1)
            v.wait_ge(s["bq_psum"], 1)
            tail(nc.vector.tensor_tensor(bias_row[:], bank(5), bias_row[:], ALU.add))
            for k in range(KC):
                tail(nc.vector.tensor_tensor(wT[:, k, P * k:P * (k + 1)], wT[:, k, P * k:P * (k + 1)], ident[:], ALU.add))
            v.wait_ge(s["mix_in"], 16 * TILES)
            with v.Fori(0, TILES) as i:
                v.wait_ge(s["f_x2p"], i)
                v.tensor_copy(x1_now, acc[:, bass.ds(i, 1), :].rearrange("p a n -> p (a n)")).then_inc(s["f_cp"], 1)
                nc.vector.tensor_copy(mix, ident[:]).then_inc(s["bd_done"], 1)
                v.wait_ge(s["bd_done"], i * (BT + 1) + 1)
                for b in range(BT):
                    r = slice(S * b, S * (b + 1))
                    nc.vector.tensor_tensor(mix[r, S * b:S * (b + 1)], ident[r, S * b:S * (b + 1)], mix_all[r, bass.ds(i, 1), :].rearrange("p a c -> p (a c)"), ALU.add).then_inc(s["bd_done"], 1)
                v.wait_ge(s["f_x3p"], i + 1)
                nc.vector.tensor_tensor(x3, bank(1), bias_row[:], ALU.add).then_inc(s["f_x3s"], 1)
                v.wait_ge(s["f_bxp"], i + 1)
                nc.vector.tensor_tensor(bx, bank(3, P), adapter[:, bass.ds(i * P, P)], ALU.mult).then_inc(s["f_bxs"], 1)
                v.wait_ge(s["f_x3s"], i + 1)
                v.wait_ge(s["f_yp"], i + 1)
                v.wait_ge(s["out_dma"], 16 * i)
                nc.vector.tensor_tensor(y, bank(4), x3, ALU.add).then_inc(s["f_out"], 1)

        @block.tensor
        def _(pe):
            mm = nc.tensor.matmul

            def project(m, part, first=False):
                if part == 0:
                    pe.wait_ge(s["xt_in"], 16 * (m + 1))
                    if not first:
                        pe.wait_ge(s["acc_done"], m - 1)
                elif part == 1:
                    if not first:
                        pe.wait_ge(s["ot_sb"], 2 * (m - 1))
                else:
                    pe.wait_ge(s["raw_a"], 2 * m + 1)
                for k in range(KC):
                    ins = mm(bank(MB if part == 1 else MA), xT[:, k, :], wqkv[:, k, 512 * part:512 * (part + 1)],
                             start=(k == 0), stop=(k == KC - 1))
                ins.then_inc(s["proj_psum"], 1)

            def keys(n, i):
                b, h = divmod(i, GH)
                if h == 0:
                    pe.wait_ge(s[f"kv_in{b}"], (n + 1) * (16 * CH))
                pe.wait_ge(s["kt_sb"], n * PAIRS + i)
                for c in range(CH):
                    ins = nc.tensor.transpose(bank(KT)[:, P * c:P * (c + 1)], kv[:, b, c, D * h:D * (h + 1)], ident[:])
                ins.then_inc(s["kt_psum"], 1)

            def queries(n, first=False):
                pe.wait_ge(s["ab_done"], n + 1)
                pe.wait_ge(s["v_sb"], n + 1)
                for j in range(REP):
                    ins = nc.tensor.transpose(bank(MA)[:, P * j:P * (j + 1)], qrope[:, j, :], ident[:])
                ins.then_inc(s["qt_psum"], 1)
                if not first:
                    pe.wait_ge(s["ot_sb"], 2 * n - 1)
                for j in range(REP):
                    ins = nc.tensor.transpose(bank(MB)[:, P * j:P * (j + 1)], qrope[:, REP + j, :], ident[:])
                ins.then_inc(s["qt_psum"], 1)
                pe.wait_ge(s["qt_sb_a"], n + 1)
                for h in range(GH):
                    ins = nc.tensor.transpose(bank(MA)[:, P * h:P * (h + 1)], qrope[:, QH + h, :], ident[:])
                ins.then_inc(s["kn_psum"], 1)

            pe.wait_ge(s["consts_in"], 16 * 3)
            for part in range(3):
                project(0, part, True)
            queries(0, True)
            keys(0, 0)

            def round_(n, last):
                for i in range(PAIRS + 2):
                    if i + 1 < PAIRS:
                        keys(n, i + 1)
                    if i < PAIRS:
                        b, h = divmod(i, GH)
                        if i == 0:
                            pe.wait_ge(s["kn_sb"], n + 1)
                            pe.wait_ge(s["qt_sb_v"], n + 1)
                        pe.wait_ge(s["kt_sb"], n * PAIRS + (i + 1))
                        pe.wait_ge(s["s_done"], n * PAIRS + i)
                        mm(bank(SC), qT[:, h, b, :], kT[:, i % 2, :], start=True, stop=True)
                        mm(bank(SC + 1, S), qT[:, h, b, :], kT_new[:, h, S * b:S * (b + 1)],
                           start=True, stop=True).then_inc(s["s_psum"], 1)
                    if 1 <= i <= PAIRS:
                        j = i - 1
                        pe.wait_ge(s["p_sb"], n * PAIRS + (j + 1))
                        pe.wait_ge(s["pt_sb"], n * PAIRS + j)
                        for c in range(CH + 1):
                            ins = nc.tensor.transpose(psum[:, 512 * PT + P * c:512 * PT + P * (c + 1)],
                                                      probs[:, j % 2, P * c:P * (c + 1)], ident[:])
                        ins.then_inc(s["pt_psum"], 1)
                    if i >= 2:
                        j = i - 2
                        b, h = divmod(j, GH)
                        if j == 0:
                            pe.wait_ge(s["vnew_in"], (n + 1) * (16 * BT))
                        if j % HALF == 0:
                            pe.wait_ge(s["o_sb"], 2 * n + j // HALF)
                        pe.wait_ge(s["pt_sb"], n * PAIRS + (j + 1))
                        for c in range(CH + 1):
                            vals = kv[:, b, c, D * (GH + h):D * (GH + h + 1)] if c < CH else v_new[:, b, D * h:D * (h + 1)]
                            ins = mm(bank(O)[:, D * (j % HALF):D * (j % HALF + 1)], pT[:, j % 2, P * c:P * (c + 1)], vals,
                                     start=(c == 0), stop=(c == CH))
                            if h == GH - 1 and c == CH - 1:
                                ins.then_inc(s[f"kv_used{b}"], 1)
                        ins.then_inc(s["pv_done"], 1)
                    if i in (0, 1, 2) and not last:
                        project(n + 1, i)
                    if i == 6:
                        if not last:
                            pe.wait_ge(s["raw_v"], n + 2)
                        outputs(n, 0)
                if not last:
                    queries(n + 1)
                    keys(n + 1, 0)
                outputs(n, 1, last)
                pe.wait_ge(s["ot_sb"], 2 * n + 2)
                if not last:
                    pe.wait_ge(s["kn_sb"], n + 2)
                for h in range(QH):
                    ins = mm(bank(MA), oT[:, h].rearrange("p b s -> p (b s)"), wo[:, h, :], start=(h == 0), stop=(h == QH - 1))
                ins.then_inc(s["wo_psum"], 1)

            def outputs(n, half, last=False):
                pe.wait_ge(s["o_sb"], 2 * n + (half + 1))
                if half and not last:
                    pe.wait_ge(s["qt_sb_v"], n + 2)
                elif half:
                    pe.wait_ge(s["ot_sb"], 2 * n + 1)
                for j in range(HALF):
                    ins = nc.tensor.transpose(bank(MB)[:, P * j:P * (j + 1)], o_nat[:, j, :], ident[:])
                ins.then_inc(s["ot_psum"], 1)

            with pe.Fori(0, ROUNDS - 1) as n:
                round_(n, False)
            round_(ROUNDS - 1, True)

            pe.wait_ge(s["wdone"], 1)
            mm(bank(5), wb, bq_f, start=True, stop=True).then_inc(s["bq_psum"], 1)
            pe.wait_ge(s["tail_p"], 5 + KC)
            with pe.Fori(0, TILES) as i:
                pe.wait_ge(s["f_cp"], i + 1)
                pe.wait_ge(s["bd_done"], (i + 1) * (BT + 1))
                pe.wait_ge(s["f_x2s"], i)
                for k in range(KC):
                    ins = mm(bank(0)[:, P * k:P * (k + 1)], x1_now[:, P * k:P * (k + 1)], mix, start=True, stop=True)
                ins.then_inc(s["f_x2p"], 1)
                pe.wait_ge(s["f_x2s"], i + 1)
                for k in range(KC):
                    ins = mm(bank(1), x2T[:, k, :], wT[:, k, :], start=(k == 0), stop=(k == KC - 1))
                ins.then_inc(s["f_x3p"], 1)
                pe.wait_ge(s["f_x3s"], i + 1)
                pe.wait_ge(s["f_x3ts"], i)
                for k in range(KC):
                    ins = nc.tensor.transpose(bank(2)[:, P * k:P * (k + 1)], x3[:, P * k:P * (k + 1)], ident[:])
                ins.then_inc(s["f_x3tp"], 1)
                pe.wait_ge(s["f_x3ts"], i + 1)
                for k in range(KC):
                    ins = mm(bank(3, P), bT[:, k, :], x3T[:, k, :], start=(k == 0), stop=(k == KC - 1))
                ins.then_inc(s["f_bxp"], 1)
                pe.wait_ge(s["f_bxs"], i + 1)
                pe.wait_ge(s["f_out"], i)
                mm(bank(4), bx, aT, start=True, stop=True).then_inc(s["f_yp"], 1)


def kernel(x, itok_Bx16_0_63, itok_B_207_1644, itok_B_0_15, condB_scale, itok_Bx4096x4096_0_255, condB_wscale,
           itok_Bx4096_0_255, condB_bscale, itok_B_3_7, _lenS, L0_cond_Wq, L0_cond_Wk, L0_cond_Wv, L0_cond_Wo,
           L0_cond_q_norm_w, L0_cond_k_norm_w, L0_cond_k_cache, L0_cond_v_cache, L1_cond_weights, L2_cond_weight,
           L2_cond_bias, L3_cond_A, L3_cond_B):
    import concourse.bacc as bacc
    from concourse.bass_utils import run_bass_kernel_spmd

    def rep(a, n=P):
        return np.broadcast_to(np.asarray(a).reshape(1, -1), (n, np.asarray(a).size))

    def by_row(a):
        a = np.asarray(a).reshape(TILES, BT, 1, -1)
        return np.broadcast_to(a, (TILES, BT, S, a.shape[-1])).reshape(TILES, P, -1).transpose(1, 0, 2)

    def weights(w, heads):
        w = np.asarray(w).reshape(GROUPS, heads // GROUPS * D, KC, P)
        return w.transpose(0, 3, 2, 1)

    x, table = np.asarray(x), np.asarray(itok_Bx16_0_63)
    pages = np.broadcast_to(table.reshape(B, CH, P // PSIZE, 1), (B, CH, P // PSIZE, PSIZE)).reshape(B * CH, P).T

    def cache(c):
        return np.asarray(c).reshape(PAGES * PSIZE, GROUPS, GH * D).transpose(1, 0, 2)

    arrays = {
        **constants(),
        "tbl_rep": pages,
        "len_rep": rep(itok_B_207_1644),
        "pos_rep": by_row(itok_B_207_1644)[:, :, 0],
        "cond_rep": by_row(itok_B_0_15)[:, :, 0],
        "scale_rep": rep(condB_scale),
        "wscale_rep": rep(condB_wscale),
        "zp_rep": rep(_lenS),
        "q_norm_rep": rep(L0_cond_q_norm_w),
        "k_norm_rep": rep(L0_cond_k_norm_w),
        "x_nat": x.reshape(TILES, P, HID).transpose(1, 0, 2),
        "xT": x.reshape(TILES, P, KC, P).transpose(0, 3, 2, 1),
        "wqkv": np.concatenate([weights(L0_cond_Wq, HQ), weights(L0_cond_Wk, HK), weights(L0_cond_Wv, HK)], axis=3),
        "wo": np.asarray(L0_cond_Wo).reshape(HID, GROUPS, QH, D).transpose(1, 3, 2, 0),
        "kv": np.concatenate([cache(L0_cond_k_cache), cache(L0_cond_v_cache)], axis=2).reshape(GROUPS * PAGES * PSIZE, -1),
        "mix": np.asarray(L1_cond_weights).reshape(CONDS * S, S),
        "weightT": np.asarray(L2_cond_weight).reshape(HID, KC, P).transpose(2, 1, 0),
        "bias_rep": rep(L2_cond_bias),
        "wq": np.asarray(itok_Bx4096x4096_0_255).reshape(B, HID, KC, P).transpose(0, 3, 2, 1).reshape(B, P, KC * HID),
        "bq": np.asarray(itok_Bx4096_0_255),
        "scale_col": np.asarray(condB_scale).reshape(B, 1),
        "bscale_col": np.asarray(condB_bscale).reshape(B, 1),
        "A_all": np.asarray(L3_cond_A).transpose(0, 2, 1).reshape(NAD * RANK, HID),
        "B_all": np.asarray(L3_cond_B).reshape(NAD * RANK, KC, P).transpose(2, 1, 0),
        "aid_rep": rep(np.repeat(np.asarray(itok_B_3_7), S)),
    }
    arrays = {k: np.ascontiguousarray(a) for k, a in arrays.items()}
    nc = bacc.Bacc("TRN2", target_bir_lowering=False, num_devices=1)
    tensors = {k: nc.dram_tensor(k, a.shape, mybir.dt.from_np(a.dtype), kind="ExternalInput").ap() for k, a in arrays.items()}
    tensors["out"] = nc.dram_tensor("out", (TILES, P, HID), F32, kind="ExternalOutput").ap()
    build(nc, tensors)
    r = run_bass_kernel_spmd(nc, [arrays], core_ids=[0])
    return r.results[0]["out"].reshape(B, S, HID)
```

```python
import numpy as np
import concourse.bass as bass
from concourse import mybir
from contextlib import ExitStack

F32 = mybir.dt.float32
I32 = mybir.dt.int32
BF16 = mybir.dt.bfloat16
ALU = mybir.AluOpType
ACT = mybir.ActivationFunctionType
AX = mybir.AxisListType

B, S, HID = 32, 32, 512
D, HQ, HK = 128, 32, 8
REP = HQ // HK
PAGES, PSIZE, NPP = 64, 32, 16
L = NPP * PSIZE
KEYS = L + S
P = 128
KC = HID // P
BT = P // S
TILES = B // BT
GH = 2
GROUPS = HK // GH
QH = GH * REP
ROUNDS = GROUPS * TILES
PAIRS = BT * GH
HALF = PAIRS // 2
CH = L // P
PCOLS = (CH + 1) * P
QKV = (QH + 2 * GH) * D
NORMED = QH + GH
CONDS, NAD, RANK = 16, 8, 16
SCALE = 1.0 / float(np.sqrt(D))
EPS = 1e-6
MASKED = -1e30
TWO_PI = 2.0 * np.pi
PI_1 = 6.28125
PI_2 = float(np.float32(np.round((TWO_PI - PI_1) * 2.0 ** 22) / 2.0 ** 22))
PI_3 = float(TWO_PI - PI_1 - PI_2)
WAVE = 4
WAVES = TILES // WAVE
TAIL_STEPS = 3 + BT + 2 + KC
ROUNDER = 1.5 * 2.0 ** 23
PI_F = 3.1415925


def constants():
    key_pos = np.concatenate([np.arange(L), np.full(S, -2.0 ** 31)]).astype(np.float32)
    inv_freq = (1.0 / np.float32(10000.0) ** (np.arange(0, D, 2, dtype=np.float32) / np.float32(D))).astype(np.float32)
    lane = np.arange(P)
    cols = np.zeros((P, 8), np.float32)
    cols[:, 0] = lane % S
    cols[:, 1] = lane // RANK
    cols[:, 2] = -0.5
    return {
        "c_ident": np.eye(P, dtype=np.float32),
        "c_key_pos": np.broadcast_to(key_pos, (P, KEYS)).copy(),
        "c_inv_freq": np.broadcast_to(inv_freq, (P, D // 2)).copy(),
        "c_cols": cols,
    }


def build(nc, t):
    ctx = ExitStack()
    with ctx:
        def sb(name, shape, dt=F32):
            return ctx.enter_context(nc.sbuf_tensor(name + "_sb", shape, dt))

        def sem(name):
            return ctx.enter_context(nc.semaphore(name))

        ident = sb("ident", [P, P])
        key_pos = sb("key_pos", [P, KEYS])
        cols = sb("cols", [P, 8])
        acc = sb("acc", [P, TILES, HID])
        wqkv = sb("wqkv", [P, KC, QKV])
        wo = sb("wo", [P, QH, HID])
        xT = sb("xT", [P, KC, P])
        qraw = sb("qraw", [P, NORMED, D])
        rope_a = sb("rope_a", [P, NORMED, D])
        rope_b = sb("rope_b", [P, NORMED, D])
        qrope = sb("qrope", [P, NORMED, D])
        ssq = sb("ssq", [P, NORMED])
        squared = sb("squared", [P, NORMED, D])
        rstd = sb("rstd", [P, NORMED])
        varr = sb("varr", [P, NORMED])
        v_nat = sb("v_nat", [P, GH * D])
        v_new = sb("v_new", [P, BT, GH * D])
        qT = sb("qT", [P, GH, BT, REP * S])
        kT_new = sb("kT_new", [P, GH, P])
        kv = sb("kv", [P, BT, CH, 2 * GH * D])
        kT = sb("kT", [P, 2, L])
        sc = sb("sc", [P, 2, KEYS])
        bias = sb("bias", [P, 2])
        probs = sb("probs", [P, 2, PCOLS])
        sums = sb("sums", [P, PAIRS])
        inv = sb("inv", [P, PAIRS])
        pT = sb("pT", [P, 2, PCOLS])
        o_nat = sb("o_nat", [P, HALF, D])
        oT = sb("oT", [P, QH, BT, S])
        page_rows = sb("page_rows", [P, GROUPS, B * CH], I32)
        rows_now = sb("rows_now", [P, BT, CH], I32)
        lens = sb("lens", [P, B])
        mask = sb("mask", [P, BT, KEYS], BF16)
        rope_c = sb("rope_c", [P, TILES, 2, D])
        rope_s = sb("rope_s", [P, TILES, 2, D])
        wT = sb("wT", [P, KC, HID])
        wq_in = sb("wq_in", [P, KC * HID], I32)
        dscale = sb("dscale", [P, B])
        small = sb("small", [P, 8, B])
        bias_row = sb("bias_row", [P, HID])

        psum = ctx.enter_context(nc.psum_tensor("psum", [P, 8 * 512], F32))

        def bank(b, n=512):
            return psum[:, 512 * b:512 * b + n]

        SC, PT, KT, O, MA, MB = 0, 2, 4, 5, 6, 7

        names = """consts_in params_in big_in rows_ready tabs_in xt_in w_in w1_in w2_in wo_in vnew_in wq_loaded
            pool_waits vector_waits sync_waits kv_in0 kv_in1 kv_in2 kv_in3 kv_used0 kv_used1 kv_used2 kv_used3 zeroed rows_now_in0 rows_now_in1 rows_now_in2 rows_now_in3 mix_in rows_v angles
            kt_psum kt_sb s_psum s_done p_sb pt_psum pt_sb pv_done o_sb ot_psum ot_sb
            qt_psum qt_sb_a qt_sb_v kn_psum kn_sb proj_psum raw_a raw_v v_sb
            sq_done ssq_done rstd_done ab_done roped rope_add mask_done lens_now_in var_done
            wo_psum acc_done dw_now dw_done chain achain
            bq_psum cond_in l1_in f_cp f_x2p f_x2s f_x3p f_x3s f_x3tp f_x3ts f_bxp f_bxs f_yp f_out out_dma bias_done wdone tail_p""".split()
        s = {n: sem(n) for n in names}

        bcol = sb("bcol", [P, 8])
        mix_all = sb("mix_all", [P, TILES, S])
        cond_i = sb("cond_i", [P, TILES], I32)
        mix_rows = sb("mix_rows", [P, TILES], I32)
        aid_i = sb("aid_i", [P, B * S], I32)

        x1_now, x2T, x3, x3T = (kv[:, j] for j in range(4))
        x2T = x2T.rearrange("p t (k n) -> p t k n", k=KC)
        x3T = x3T.rearrange("p t (k n) -> p t k n", k=KC)
        y = wo[:, 0:WAVE, :]
        bx = wo[:, WAVE, :].rearrange("p (t n) -> p t n", t=WAVE)
        mix = aid_i[:].bitcast(F32).rearrange("p (t n) -> p t n", t=TILES)
        bT = wqkv[:, 0, 0:KC * P].rearrange("p (k r) -> p k r", k=KC)
        aT = wqkv[:, 1, 0:HID]
        adapter = wqkv[:, 2, 0:B * S]
        bq_i = wqkv[0:B, 3, 0:HID].bitcast(I32)
        bq_f = wqkv[0:B, 3, HID:2 * HID]
        wb = wqkv[0:B, 3, 2 * HID:2 * HID + P]

        block = ctx.enter_context(nc.Block())

        @block.sync
        def _(sp):
            sp.dma_start(cols[:], t["c_cols"]).then_inc(s["params_in"], 16)
            sp.dma_start(kT[:, 0, 0:B * CH].bitcast(I32), t["tbl_rep"]).then_inc(s["params_in"], 16)
            sp.dma_start(small[:, 0, :].bitcast(I32), t["len_rep"]).then_inc(s["params_in"], 16)
            sp.dma_start(small[:, 1, 0:TILES].bitcast(I32), t["pos_rep"]).then_inc(s["params_in"], 16)
            sp.dma_start(cond_i[:], t["cond_rep"]).then_inc(s["params_in"], 16)
            sp.dma_start(rope_a[:, 0, 0:D // 2], t["c_inv_freq"]).then_inc(s["params_in"], 16)
            sp.dma_start(rope_a[:, 1, :], t["q_norm_rep"]).then_inc(s["params_in"], 16)
            sp.dma_start(rope_a[:, 2, :], t["k_norm_rep"]).then_inc(s["params_in"], 16)
            sp.dma_start(xT[:], t["xT"][0]).then_inc(s["xt_in"], 16)
            for part in range(3):
                cs = slice(512 * part, 512 * (part + 1))
                sp.dma_start(wqkv[:, :, cs], t["wqkv"][0][:, :, cs]).then_inc(s[("w_in", "w1_in", "w2_in")[part]], 16)
            sp.dma_start(ident[:], t["c_ident"]).then_inc(s["consts_in"], 16)
            sp.dma_start(key_pos[:], t["c_key_pos"]).then_inc(s["big_in"], 16)
            sp.dma_start(small[:, 2, :], t["scale_rep"]).then_inc(s["big_in"], 16)
            sp.dma_start(small[:, 3, :], t["wscale_rep"]).then_inc(s["big_in"], 16)
            sp.dma_start(small[:, 4, :].bitcast(I32), t["zp_rep"]).then_inc(s["big_in"], 16)
            sp.dma_start(wT[:], t["weightT"]).then_inc(s["big_in"], 16)
            sp.dma_start(bias_row[:], t["bias_rep"]).then_inc(s["big_in"], 16)
            sp.dma_start(acc[:], t["x_nat"]).then_inc(s["big_in"], 16)
            sp.dma_start(wo[:], t["wo"][0]).then_inc(s["wo_in"], 16)
            sp.wait_ge(s["zeroed"], 2)

            def load_round(m, i):
                sp.wait_ge(s["proj_psum"], m * 3)
                sp.sem_inc(s["sync_waits"], 1)
                sp.dma_start(xT[:], t["xT"][bass.ds(i, 1)].rearrange("a p k n -> p (a k) n")).then_inc(s["xt_in"], 16)
                deltas_and_values(m - 1)

            def deltas_and_values(m):
                sp.wait_ge(s["dw_done"], m)
                sp.sem_inc(s["sync_waits"], 1)
                sp.dma_start(wq_in[:], t["wq"][bass.ds(m, 1)].rearrange("a p n -> (a p) n")).then_inc(s["wq_loaded"], 16)
                sp.wait_ge(s["v_sb"], m + 1)
                sp.sem_inc(s["sync_waits"], 1)
                sp.wait_ge(s["pv_done"], m * PAIRS)
                sp.sem_inc(s["sync_waits"], 1)
                for b in range(BT):
                    sp.dma_start(v_new[0:S, b, :], v_nat[S * b:S * (b + 1), :]).then_inc(s["vnew_in"], 16)

            with sp.Fori(1, TILES) as i:
                load_round(i, i)
            with sp.Fori(1, GROUPS) as g:
                sp.wait_ge(s["proj_psum"], g * (3 * TILES))
                sp.sem_inc(s["sync_waits"], 1)
                sp.dma_start(wqkv[:], t["wqkv"][bass.ds(g, 1)].rearrange("a p k n -> p (a k) n")).then_inc(s["w_in"], 16)
                sp.wait_ge(s["w_in"], g * 16 + 16)
                sp.sem_inc(s["sync_waits"], 1)
                load_round(g * TILES, 0)
                load_round(g * TILES + 1, 1)
                sp.wait_ge(s["wo_psum"], g * TILES)
                sp.sem_inc(s["sync_waits"], 1)
                sp.dma_start(wo[:], t["wo"][bass.ds(g, 1)].rearrange("a p h n -> p (a h) n")).then_inc(s["wo_in"], 16)
                with sp.Fori(2, TILES) as i:
                    load_round(g * TILES + i, i)
            deltas_and_values(ROUNDS - 1)
            sp.wait_ge(s["proj_psum"], 3 * ROUNDS)
            sp.dma_start(bT, t["B_all"]).then_inc(s["tabs_in"], 16)
            sp.dma_start(aT, t["A_all"]).then_inc(s["tabs_in"], 16)
            sp.dma_start(aid_i[:], t["aid_rep"]).then_inc(s["tabs_in"], 16)
            sp.dma_start(bq_i, t["bq"]).then_inc(s["tabs_in"], 16)
            sp.dma_start(bcol[0:B, 0:1], t["scale_col"]).then_inc(s["tabs_in"], 16)
            sp.dma_start(bcol[0:B, 1:2], t["bscale_col"]).then_inc(s["tabs_in"], 16)
            with sp.Fori(0, WAVES) as w:
                for j in range(WAVE):
                    sp.wait_ge(s["f_out"], w * WAVE + (j + 1))
                    sp.sem_inc(s["sync_waits"], 1)
                    sp.dma_start(t["out"][bass.ds(w * WAVE + j, 1)].rearrange("a p n -> (a p) n"), y[:, j, :]).then_inc(s["out_dma"], 16)
            sp.wait_ge(s["out_dma"], 16 * TILES)

        @block.gpsimd
        def _(po):
            po.memset(probs[:], 0.0).then_inc(s["zeroed"], 1)
            po.memset(v_new[:], 0.0).then_inc(s["zeroed"], 1)
            po.wait_ge(s["rows_ready"], 1)
            rows = page_rows[:].rearrange("p g c -> p (g c)")

            def inverse_root(m1):
                po.wait_ge(s["ssq_done"], m1)
                po.sem_inc(s["pool_waits"], 1)
                po.tensor_scalar(varr[:], ssq[:], 1.0 / D, EPS, ALU.mult, ALU.add).then_inc(s["var_done"], 1)
                po.wait_ge(s["var_done"], m1)
                po.sem_inc(s["pool_waits"], 1)
                po.tensor_tensor(rstd[:], varr[:], cols[:, 2:3].to_broadcast([P, NORMED]), ALU.pow).then_inc(s["rstd_done"], 1)

            def gather(n, first=False):
                for b in range(BT):
                    if not first:
                        po.wait_ge(s[f"kv_used{b}"], n - 1)
                        po.sem_inc(s["pool_waits"], 1)
                    po.tensor_copy(rows_now[:, b, :], rows[:, bass.ds((n - 1) * (BT * CH) + b * CH, CH)]
                                   ).then_inc(s[f"rows_now_in{b}"], 1)
                    po.wait_ge(s[f"rows_now_in{b}"], n)
                    po.sem_inc(s["pool_waits"], 1)
                    for c in range(CH):
                        po.indirect_dma_start(out=kv[:, b, c, :], out_offset=None, in_=t["kv"],
                                              in_offset=bass.IndirectOffsetOnAxis(ap=rows_now[:, b, c:c + 1], axis=0)
                                              ).then_inc(s[f"kv_in{b}"], 16)

            gather(1, True)
            for i in range(TILES):
                po.indirect_dma_start(out=mix_all[:, i, :], out_offset=None, in_=t["mix"],
                                      in_offset=bass.IndirectOffsetOnAxis(ap=mix_rows[:, i:i + 1], axis=0)
                                      ).then_inc(s["mix_in"], 16)
            inverse_root(1)
            inverse_root(2)
            with po.Fori(2, ROUNDS) as n:
                gather(n)
                inverse_root(n + 1)
            gather(ROUNDS)

        @block.scalar
        def _(act):
            sin_t = qrope[:, 0:4, :].rearrange("p h d -> p (h d)")
            cos_t = qrope[:, 4:8, :].rearrange("p h d -> p (h d)")
            act.wait_ge(s["angles"], 1)
            nc.scalar.activation(sin_t, sin_t, ACT.Sin)
            nc.scalar.activation(cos_t, cos_t, ACT.Sin).then_inc(s["achain"], 1)

            def take_proj(m, first=False):
                act.wait_ge(s["proj_psum"], 3 * m + 1)
                if not first:
                    act.wait_ge(s["roped"], m)
                nc.scalar.copy(qraw[:, 0:REP, :].rearrange("p h d -> p (h d)"), bank(MA)).then_inc(s["raw_a"], 1)

            def take_kv(m, first=False):
                act.wait_ge(s["proj_psum"], 3 * m + 3)
                nc.scalar.copy(qraw[:, QH:NORMED, :].rearrange("p h d -> p (h d)"), bank(MA, GH * D)).then_inc(s["raw_a"], 1)
                if not first:
                    act.wait_ge(s["vnew_in"], m * (16 * BT))
                nc.scalar.copy(v_nat[:], psum[:, 512 * MA + GH * D:512 * (MA + 1)]).then_inc(s["v_sb"], 1)

            def squares(m):
                act.wait_ge(s["raw_v"], m + 1)
                act.wait_ge(s["raw_a"], 2 * m + 2)
                act.wait_ge(s["rstd_done"], m)
                for h in range(NORMED):
                    ins = nc.scalar.activation(squared[:, h, :], qraw[:, h, :], ACT.Square, accum_out=ssq[:, h:h + 1])
                ins.then_inc(s["ssq_done"], 1)

            def take_queries(n):
                act.wait_ge(s["qt_psum"], 2 * n + 1)
                nc.scalar.copy(qT[:, 0].rearrange("p b (j s) -> p j b s", j=REP),
                               bank(MA).rearrange("p (j b s) -> p j b s", j=REP, b=BT)).then_inc(s["qt_sb_a"], 1)
                act.wait_ge(s["kn_psum"], n + 1)
                nc.scalar.copy(kT_new[:].rearrange("p h k -> p (h k)"), bank(MA, GH * P)).then_inc(s["kn_sb"], 1)

            def keys(n, i):
                act.wait_ge(s["kt_psum"], n * PAIRS + (i + 1))
                nc.scalar.copy(kT[:, i % 2, :], bank(KT)).then_inc(s["kt_sb"], 1)

            take_proj(0, True)
            take_kv(0, True)
            squares(0)
            take_queries(0)
            keys(0, 0)

            def round_(n, last):
                for i in range(PAIRS + 2):
                    if i + 1 < PAIRS:
                        keys(n, i + 1)
                    if i < PAIRS:
                        act.wait_ge(s["s_done"], n * PAIRS + (i + 1))
                        act.wait_ge(s["pt_psum"], n * PAIRS + (i - 1 if i >= 2 else 0))
                        nc.scalar.activation(probs[:, i % 2, 0:KEYS], sc[:, i % 2, :], ACT.Exp, bias=bias[:, i % 2:i % 2 + 1],
                                             scale=-1.0, accum_out=sums[:, i:i + 1]).then_inc(s["p_sb"], 1)
                    if i == 1 and not last:
                        take_proj(n + 1)
                    if i == 3 and not last:
                        take_kv(n + 1)
                    if i == 4 and not last:
                        squares(n + 1)
                    if i == 6:
                        take_outputs(n, 0)
                if not last:
                    take_queries(n + 1)
                    keys(n + 1, 0)
                take_outputs(n, 1)

            def take_outputs(n, half):
                act.wait_ge(s["ot_psum"], 2 * n + (half + 1))
                nb = BT // 2
                nc.scalar.copy(oT[:, :, nb * half:nb * (half + 1), :].rearrange("p h b s -> p b h s"),
                               bank(MB).rearrange("p (b h s) -> p b h s", b=nb, h=QH)).then_inc(s["ot_sb"], 1)

            with act.Fori(0, ROUNDS - 1) as n:
                round_(n, False)
            round_(ROUNDS - 1, True)

            act.wait_ge(s["pv_done"], ROUNDS * PAIRS)
            with act.Fori(0, WAVES) as w:
                act.wait_ge(s["acc_done"], w + (ROUNDS - WAVES + 1))
                act.wait_ge(s["f_x2p"], w * WAVE)
                for j in range(WAVE):
                    nc.scalar.copy(x1_now[:, j, :], acc[:, bass.ds(w * WAVE + j, 1), :].rearrange("p a n -> p (a n)")).then_inc(s["f_cp"], 1)
                for j in range(WAVE):
                    act.wait_ge(s["f_x2p"], w * WAVE + (j + 1))
                    nc.scalar.copy(x2T[:, j].rearrange("p k n -> p (k n)"), bank(j % 2)).then_inc(s["f_x2s"], 1)
                for j in range(WAVE):
                    act.wait_ge(s["f_x3tp"], w * WAVE + (j + 1))
                    nc.scalar.copy(x3T[:, j].rearrange("p k n -> p (k n)"), bank(4 + j % 2)).then_inc(s["f_x3ts"], 1)

        @block.vector
        def _(v):
            link = [0]

            def chained(ins):
                link[0] += 1
                ins.then_inc(s["chain"], 1)
                v.wait_ge(s["chain"], link[0])

            v.wait_ge(s["params_in"], 16 * 8)
            tbl = kT[:, 0, 0:B * CH].bitcast(I32)
            row_f = kT[:, 1, 0:B * CH]
            chained(nc.vector.tensor_scalar(row_f, tbl, float(PSIZE), cols[:, 0:1], ALU.mult, ALU.add))
            for g in range(GROUPS):
                chained(nc.vector.tensor_scalar(page_rows[:, g, :], row_f, float(g * PAGES * PSIZE), None, ALU.add))
            chained(nc.vector.tensor_copy(small[:, 5, 0:TILES], cond_i[:]))
            chained(nc.vector.tensor_scalar(mix_rows[:], small[:, 5, 0:TILES], float(S), cols[:, 0:1], ALU.mult, ALU.add))
            nc.vector.tensor_copy(lens[:], small[:, 0, :].bitcast(I32)).then_inc(s["rows_ready"], 1)
            v.wait_ge(s["rows_ready"], 1)
            pos_i = small[:, 1, 0:TILES].bitcast(I32)
            chained(nc.vector.tensor_copy(small[:, 5, 0:TILES], pos_i))
            chained(nc.vector.tensor_scalar(small[:, 6, 0:TILES], small[:, 5, 0:TILES], cols[:, 0:1], None, ALU.add))
            HD = D // 2
            ang = rope_b[:, 0:4, :].rearrange("p h d -> p (h d)")
            turns = rope_b[:, 4:8, :].rearrange("p h d -> p (h d)")
            for i in range(TILES):
                chained(nc.vector.tensor_scalar(ang[:, HD * i:HD * (i + 1)], rope_a[:, 0, 0:HD], small[:, 6, i:i + 1], None, ALU.mult))
            for quarter, dst in ((0.0, qrope[:, 0:4, :]), (0.25, qrope[:, 4:8, :])):
                r = dst.rearrange("p h d -> p (h d)")
                chained(nc.vector.tensor_scalar(turns, ang, 1.0 / TWO_PI, quarter, ALU.mult, ALU.add))
                chained(nc.vector.tensor_scalar(turns, turns, ROUNDER, None, ALU.add))
                chained(nc.vector.tensor_scalar(turns, turns, -ROUNDER, None, ALU.add))
                chained(nc.vector.scalar_tensor_tensor(r, turns, -PI_1, ang, ALU.mult, ALU.add))
                chained(nc.vector.scalar_tensor_tensor(r, turns, -PI_2, r, ALU.mult, ALU.add))
                chained(nc.vector.scalar_tensor_tensor(r, turns, -PI_3, r, ALU.mult, ALU.add))
                if quarter:
                    chained(nc.vector.tensor_scalar(r, r, TWO_PI / 4, None, ALU.add))
                ins = nc.vector.tensor_scalar(r, r, PI_F, -PI_F, ALU.min, ALU.max)
                if not quarter:
                    chained(ins)
            ins.then_inc(s["angles"], 1)
            v.wait_ge(s["achain"], 1)
            sin_t = qrope[:, 0:4, :].rearrange("p h d -> p (h d)").rearrange("p (t d) -> p t d", t=TILES)
            cos_t = qrope[:, 4:8, :].rearrange("p h d -> p (h d)").rearrange("p (t d) -> p t d", t=TILES)
            for kind in range(2):
                w1 = rope_a[:, 1 + kind, 0:HD].unsqueeze(1).to_broadcast([P, TILES, HD])
                w2 = rope_a[:, 1 + kind, HD:D].unsqueeze(1).to_broadcast([P, TILES, HD])
                chained(nc.vector.tensor_tensor(rope_c[:, :, kind, 0:HD], cos_t, w1, ALU.mult))
                chained(nc.vector.tensor_tensor(rope_c[:, :, kind, HD:D], cos_t, w2, ALU.mult))
                chained(nc.vector.scalar_tensor_tensor(rope_s[:, :, kind, 0:HD], sin_t, -1.0, w2, ALU.mult, ALU.mult))
                chained(nc.vector.tensor_tensor(rope_s[:, :, kind, HD:D], sin_t, w1, ALU.mult))

            def delta_scales():
                v.wait_ge(s["big_in"], 16 * 7)
                chained(nc.vector.tensor_tensor(dscale[:], small[:, 2, :], small[:, 3, :], ALU.mult))
                chained(nc.vector.tensor_copy(small[:, 5, :], small[:, 4, :].bitcast(I32)))
                chained(nc.vector.tensor_tensor(small[:, 6, :], small[:, 5, :], small[:, 2, :], ALU.mult))
                chained(nc.vector.tensor_reduce(small[:, 7, 0:1], small[:, 6, :], AX.X, ALU.add))
                chained(nc.vector.tensor_scalar(wT[:], wT[:], small[:, 7, 0:1], None, ALU.add))
                chained(nc.vector.tensor_scalar(bias_row[:], bias_row[:], small[:, 7, 0:1], None, ALU.add))

            def take_proj(m, first=False):
                v.wait_ge(s["proj_psum"], 3 * m + 2)
                if not first:
                    v.wait_ge(s["roped"], m)
                nc.vector.tensor_copy(qraw[:, REP:QH, :].rearrange("p h d -> p (h d)"), bank(MB)).then_inc(s["raw_v"], 1)

            def rotate(m, tile):
                v.wait_ge(s["raw_a"], 2 * m + 2)
                v.wait_ge(s["raw_v"], m + 1)
                v.wait_ge(s["ab_done"], m)
                for kind, lo, hi in ((0, 0, QH), (1, QH, NORMED)):
                    n_h = hi - lo
                    c = rope_c[:, tile, kind, :].rearrange("p a d -> p (a d)").unsqueeze(1).to_broadcast([P, n_h, D])
                    nc.vector.tensor_tensor(rope_a[:, lo:hi, :], qraw[:, lo:hi, :], c, ALU.mult)
                    for half in range(2):
                        other = 1 - half
                        sn = rope_s[:, tile, kind, HD * half:HD * (half + 1)].rearrange("p a d -> p (a d)").unsqueeze(1).to_broadcast([P, n_h, HD])
                        ins = nc.vector.tensor_tensor(rope_b[:, lo:hi, HD * half:HD * (half + 1)],
                                                      qraw[:, lo:hi, HD * other:HD * (other + 1)], sn, ALU.mult)
                ins.then_inc(s["roped"], 1)

            def add_halves(m):
                v.wait_ge(s["roped"], m + 1)
                nc.vector.tensor_tensor(rope_a[:], rope_a[:], rope_b[:], ALU.add).then_inc(s["rope_add"], 1)

            def normalise(m):
                v.wait_ge(s["rstd_done"], m + 1)
                v.wait_ge(s["rope_add"], m + 1)
                v.wait_ge(s["kn_psum"], m)
                nc.vector.tensor_tensor(qrope[:], rope_a[:], rstd[:].unsqueeze(2).to_broadcast([P, NORMED, D]),
                                        ALU.mult).then_inc(s["ab_done"], 1)

            def take_queries(n):
                v.wait_ge(s["qt_psum"], 2 * n + 2)
                nc.vector.tensor_copy(qT[:, 1].rearrange("p b (j s) -> p j b s", j=REP),
                                      bank(MB).rearrange("p (j b s) -> p j b s", j=REP, b=BT)).then_inc(s["qt_sb_v"], 1)

            def set_mask(b, batch):
                nc.vector.tensor_scalar(mask[:, b, :], key_pos[:], lens[:, batch], MASKED, ALU.is_ge, ALU.mult).then_inc(s["mask_done"], 1)

            take_proj(0, True)
            rotate(0, slice(0, 1))
            add_halves(0)
            v.wait_ge(s["big_in"], 16 * 7)
            for b in range(BT):
                set_mask(b, slice(b, b + 1))
            normalise(0)
            take_queries(0)

            def add_output(n):
                v.wait_ge(s["wo_psum"], n + 1)
                a = acc[:, bass.ds(n % TILES, 1), :].rearrange("p a n -> p (a n)")
                nc.vector.tensor_tensor(a, bank(MB), a, ALU.add).then_inc(s["acc_done"], 1)

            def round_(n, next_tile, last, first=False):
                for i in range(PAIRS + 2):
                    if i < PAIRS:
                        if i % GH == 0:
                            v.wait_ge(s["mask_done"], n * BT + (i // GH + 1))
                        if i >= 2:
                            v.wait_ge(s["p_sb"], n * PAIRS + (i - 1))
                        else:
                            v.wait_ge(s["p_sb"], n * PAIRS)
                        v.wait_ge(s["s_psum"], n * PAIRS + (i + 1))
                        v.sem_inc(s["vector_waits"], 1)
                        nc.vector.tensor_tensor_reduce(out=sc[:, i % 2, :], in0=psum[:, 512 * SC:512 * SC + KEYS],
                                                       in1=mask[:, i // GH, :], scale=-SCALE, scalar=3e38,
                                                       op0=ALU.add, op1=ALU.min,
                                                       accum_out=bias[:, i % 2:i % 2 + 1]).then_inc(s["s_done"], 1)
                    if 1 <= i <= PAIRS:
                        j = i - 1
                        if j >= 2:
                            v.wait_ge(s["pv_done"], n * PAIRS + (j - 1))
                        else:
                            v.wait_ge(s["pv_done"], n * PAIRS)
                        v.wait_ge(s["pt_psum"], n * PAIRS + (j + 1))
                        nc.vector.tensor_copy(pT[:, j % 2, :], psum[:, 512 * PT:512 * PT + PCOLS]).then_inc(s["pt_sb"], 1)
                    if not last and i >= 2 and i % GH == 0:
                        b = i // GH - 1
                        set_mask(b, bass.ds((n + 1) % TILES * BT + b, 1))
                    if i == 0:
                        if first:
                            delta_scales()
                        else:
                            v.wait_ge(s["dw_done"], n)
                        v.wait_ge(s["wq_loaded"], 16 * (n + 1))
                        wflat = wT[:].rearrange("p k n -> p (k n)")
                        nc.vector.scalar_tensor_tensor(wflat, wq_in[:], dscale[:, bass.ds(n, 1)], wflat, ALU.mult, ALU.add).then_inc(s["dw_done"], 1)
                        if not first:
                            add_output(n - 1)
                    if i == 3 and not last:
                        take_proj(n + 1)
                    if i == 4 and not last:
                        rotate(n + 1, next_tile)
                    if i == 5 and not last:
                        add_halves(n + 1)
                    if i == 5:
                        outputs(n, 0)
                    if i == 7 and not last:
                        normalise(n + 1)
                    if i == 3 and last:
                        prepare_tail()
                outputs(n, 1)
                if not last:
                    take_queries(n + 1)

            def outputs(n, half):
                v.wait_ge(s["p_sb"], n * PAIRS + HALF * (half + 1))
                nc.vector.reciprocal(inv[:, HALF * half:HALF * (half + 1)], sums[:, HALF * half:HALF * (half + 1)]).then_inc(s["rows_v"], 1)
                v.wait_ge(s["rows_v"], 2 * n + (half + 1))
                v.wait_ge(s["pv_done"], n * PAIRS + HALF * (half + 1))
                nc.vector.tensor_tensor(o_nat[:], bank(O).rearrange("p (i d) -> p i d", i=HALF),
                                        inv[:, HALF * half:HALF * (half + 1)].unsqueeze(2).to_broadcast([P, HALF, D]),
                                        ALU.mult).then_inc(s["o_sb"], 1)

            prepared = [0]

            def prepare(ins):
                prepared[0] += 1
                ins.then_inc(s["tail_p"], 1)
                v.wait_ge(s["tail_p"], prepared[0])

            def prepare_tail():
                v.wait_ge(s["tabs_in"], 16 * 6)
                prepare(nc.vector.tensor_copy(adapter, aid_i[:]))
                prepare(nc.vector.tensor_scalar(adapter, adapter, cols[:, 1:2], None, ALU.is_equal))
                v.wait_ge(s["mix_in"], 16 * TILES)
                prepare(nc.vector.tensor_copy(mix, ident[:].unsqueeze(1).to_broadcast([P, TILES, P])))
                for b in range(BT):
                    r = slice(S * b, S * (b + 1))
                    prepare(nc.vector.tensor_tensor(mix[r, :, S * b:S * (b + 1)], mix_all[r],
                                                    ident[r, S * b:S * (b + 1)].unsqueeze(1).to_broadcast([S, TILES, S]), ALU.add))
                prepare(nc.vector.tensor_copy(bq_f, bq_i))
                prepare(nc.vector.tensor_tensor(bcol[0:B, 3:4], bcol[0:B, 0:1], bcol[0:B, 1:2], ALU.mult))
                nc.vector.tensor_copy(wb, bcol[0:B, 3:4].to_broadcast([B, P])).then_inc(s["wdone"], 1)

            round_(0, slice(1, 2), False, True)
            with v.Fori(1, ROUNDS - 1) as n:
                round_(n, bass.ds((n + 1) % TILES, 1), False)
            round_(ROUNDS - 1, None, True)

            for k in range(KC):
                prepare(nc.vector.tensor_tensor(wT[:, k, P * k:P * (k + 1)], wT[:, k, P * k:P * (k + 1)], ident[:], ALU.add))
            add_output(ROUNDS - 1)
            v.wait_ge(s["bq_psum"], 1)
            prepare(nc.vector.tensor_tensor(bias_row[:], bank(5), bias_row[:], ALU.add))
            with v.Fori(0, WAVES) as w:
                for j in range(WAVE):
                    v.wait_ge(s["f_x3p"], w * WAVE + (j + 1))
                    nc.vector.tensor_tensor(x3[:, j, :], bank(2 + j % 2), bias_row[:], ALU.add).then_inc(s["f_x3s"], 1)
                v.wait_ge(s["f_bxp"], w + 1)
                nc.vector.tensor_tensor(bx.rearrange("p t n -> p (t n)"), bank(6), adapter[:, bass.ds(w * (WAVE * P), WAVE * P)],
                                        ALU.mult).then_inc(s["f_bxs"], 1)
                v.wait_ge(s["f_x3s"], (w + 1) * WAVE)
                v.wait_ge(s["out_dma"], w * (16 * WAVE))
                for j in range(WAVE):
                    v.wait_ge(s["f_yp"], w * WAVE + (j + 1))
                    nc.vector.tensor_tensor(y[:, j, :], bank(7 - j % 2), x3[:, j, :], ALU.add).then_inc(s["f_out"], 1)

        @block.tensor
        def _(pe):
            mm = nc.tensor.matmul

            def project(m, part, first=False, second=False):
                if first:
                    pe.wait_ge(s[("w_in", "w1_in", "w2_in")[part]], 16)
                if part == 0:
                    pe.wait_ge(s["xt_in"], 16 * (m + 1))
                elif part == 1:
                    if not (first or second):
                        pe.wait_ge(s["acc_done"], m - 1)
                else:
                    pe.wait_ge(s["raw_a"], 2 * m + 1)
                for k in range(KC):
                    ins = mm(bank(MB if part == 1 else MA), xT[:, k, :], wqkv[:, k, 512 * part:512 * (part + 1)],
                             start=(k == 0), stop=(k == KC - 1))
                ins.then_inc(s["proj_psum"], 1)

            def keys(n, i):
                b, h = divmod(i, GH)
                if h == 0:
                    pe.wait_ge(s[f"kv_in{b}"], (n + 1) * (16 * CH))
                pe.wait_ge(s["kt_sb"], n * PAIRS + i)
                for c in range(CH):
                    ins = nc.tensor.transpose(bank(KT)[:, P * c:P * (c + 1)], kv[:, b, c, D * h:D * (h + 1)], ident[:])
                ins.then_inc(s["kt_psum"], 1)

            def queries(n, first=False):
                pe.wait_ge(s["ab_done"], n + 1)
                pe.wait_ge(s["v_sb"], n + 1)
                for j in range(REP):
                    ins = nc.tensor.transpose(bank(MA)[:, P * j:P * (j + 1)], qrope[:, j, :], ident[:])
                ins.then_inc(s["qt_psum"], 1)
                if not first:
                    pe.wait_ge(s["ot_sb"], 2 * n - 1)
                for j in range(REP):
                    ins = nc.tensor.transpose(bank(MB)[:, P * j:P * (j + 1)], qrope[:, REP + j, :], ident[:])
                ins.then_inc(s["qt_psum"], 1)
                pe.wait_ge(s["qt_sb_a"], n + 1)
                for h in range(GH):
                    ins = nc.tensor.transpose(bank(MA)[:, P * h:P * (h + 1)], qrope[:, QH + h, :], ident[:])
                ins.then_inc(s["kn_psum"], 1)

            for part in range(3):
                project(0, part, True)
            pe.wait_ge(s["consts_in"], 16)
            queries(0, True)
            keys(0, 0)

            def round_(n, last, first=False):
                for i in range(PAIRS + 2):
                    if i + 1 < PAIRS:
                        keys(n, i + 1)
                    if i < PAIRS:
                        b, h = divmod(i, GH)
                        if i == 0:
                            pe.wait_ge(s["kn_sb"], n + 1)
                            pe.wait_ge(s["qt_sb_v"], n + 1)
                        pe.wait_ge(s["kt_sb"], n * PAIRS + (i + 1))
                        pe.wait_ge(s["s_done"], n * PAIRS + i)
                        mm(bank(SC), qT[:, h, b, :], kT[:, i % 2, :], start=True, stop=True)
                        mm(bank(SC + 1, S), qT[:, h, b, :], kT_new[:, h, S * b:S * (b + 1)],
                           start=True, stop=True).then_inc(s["s_psum"], 1)
                    if 1 <= i <= PAIRS:
                        j = i - 1
                        pe.wait_ge(s["p_sb"], n * PAIRS + (j + 1))
                        pe.wait_ge(s["pt_sb"], n * PAIRS + j)
                        for c in range(CH + 1):
                            ins = nc.tensor.transpose(psum[:, 512 * PT + P * c:512 * PT + P * (c + 1)],
                                                      probs[:, j % 2, P * c:P * (c + 1)], ident[:])
                        ins.then_inc(s["pt_psum"], 1)
                    if i >= 2:
                        j = i - 2
                        b, h = divmod(j, GH)
                        if j == 0:
                            pe.wait_ge(s["vnew_in"], (n + 1) * (16 * BT))
                        if j % HALF == 0:
                            pe.wait_ge(s["o_sb"], 2 * n + j // HALF)
                        pe.wait_ge(s["pt_sb"], n * PAIRS + (j + 1))
                        for c in range(CH + 1):
                            vals = kv[:, b, c, D * (GH + h):D * (GH + h + 1)] if c < CH else v_new[:, b, D * h:D * (h + 1)]
                            ins = mm(bank(O)[:, D * (j % HALF):D * (j % HALF + 1)], pT[:, j % 2, P * c:P * (c + 1)], vals,
                                     start=(c == 0), stop=(c == CH))
                            if h == GH - 1 and c == CH - 1:
                                ins.then_inc(s[f"kv_used{b}"], 1)
                        ins.then_inc(s["pv_done"], 1)
                    if i == 0 and not first:
                        output_projection(n - 1)
                    if i in (1, 2, 3) and not last:
                        project(n + 1, i - 1, False) if not first else project(1, i - 1, False, True)
                    if i == 6:
                        if not last:
                            pe.wait_ge(s["raw_v"], n + 2)
                        outputs(n, 0)
                if not last:
                    queries(n + 1)
                    keys(n + 1, 0)
                outputs(n, 1, last)

            def output_projection(n):
                pe.wait_ge(s["ot_sb"], 2 * n + 2)
                pe.wait_ge(s["wo_in"], (n // TILES + 1) * 16)
                for h in range(QH):
                    ins = mm(bank(MB), oT[:, h].rearrange("p b s -> p (b s)"), wo[:, h, :], start=(h == 0), stop=(h == QH - 1))
                ins.then_inc(s["wo_psum"], 1)

            def outputs(n, half, last=False):
                pe.wait_ge(s["o_sb"], 2 * n + (half + 1))
                if half and not last:
                    pe.wait_ge(s["qt_sb_v"], n + 2)
                elif half:
                    pe.wait_ge(s["ot_sb"], 2 * n + 1)
                for j in range(HALF):
                    ins = nc.tensor.transpose(bank(MB)[:, P * j:P * (j + 1)], o_nat[:, j, :], ident[:])
                ins.then_inc(s["ot_psum"], 1)

            round_(0, False, True)
            with pe.Fori(1, ROUNDS - 1) as n:
                round_(n, False)
            round_(ROUNDS - 1, True)
            output_projection(ROUNDS - 1)

            pe.wait_ge(s["wdone"], 1)
            pe.wait_ge(s["pt_sb"], ROUNDS * PAIRS)
            pe.wait_ge(s["o_sb"], 2 * ROUNDS)
            mm(bank(5), wb, bq_f, start=True, stop=True).then_inc(s["bq_psum"], 1)
            with pe.Fori(0, WAVES) as w:
                for j in range(WAVE):
                    pe.wait_ge(s["f_cp"], w * WAVE + (j + 1))
                    if j >= 2:
                        pe.wait_ge(s["f_x2s"], w * WAVE + (j - 1))
                    for k in range(KC):
                        ins = mm(bank(j % 2)[:, P * k:P * (k + 1)], x1_now[:, j, P * k:P * (k + 1)],
                                 mix[:, bass.ds(w * WAVE + j, 1), :].rearrange("p a n -> p (a n)"), start=True, stop=True)
                    ins.then_inc(s["f_x2p"], 1)
                pe.wait_ge(s["tail_p"], TAIL_STEPS)
                for j in range(WAVE):
                    pe.wait_ge(s["f_x2s"], w * WAVE + (j + 1))
                    if j >= 2:
                        pe.wait_ge(s["f_x3s"], w * WAVE + (j - 1))
                    for k in range(KC):
                        ins = mm(bank(2 + j % 2), x2T[:, j, k, :], wT[:, k, :], start=(k == 0), stop=(k == KC - 1))
                    ins.then_inc(s["f_x3p"], 1)
                for j in range(WAVE):
                    pe.wait_ge(s["f_x3s"], w * WAVE + (j + 1))
                    if j >= 2:
                        pe.wait_ge(s["f_x3ts"], w * WAVE + (j - 1))
                    for k in range(KC):
                        ins = nc.tensor.transpose(bank(4 + j % 2)[:, P * k:P * (k + 1)], x3[:, j, P * k:P * (k + 1)], ident[:])
                    ins.then_inc(s["f_x3tp"], 1)
                for j in range(WAVE):
                    pe.wait_ge(s["f_x3ts"], w * WAVE + (j + 1))
                    if j == 0:
                        pe.wait_ge(s["f_out"], w * WAVE)
                    for k in range(KC):
                        ins = mm(bank(6)[:, P * j:P * (j + 1)], bT[:, k, :], x3T[:, j, k, :], start=(k == 0), stop=(k == KC - 1))
                ins.then_inc(s["f_bxp"], 1)
                pe.wait_ge(s["f_bxs"], w + 1)
                for j in range(WAVE):
                    if j >= 2:
                        pe.wait_ge(s["f_out"], w * WAVE + (j - 1))
                    mm(bank(7 - j % 2), bx[:, j, :], aT, start=True, stop=True).then_inc(s["f_yp"], 1)


def kernel(x, itok_Bx16_0_63, itok_B_207_1644, itok_B_0_15, condB_scale, itok_Bx4096x4096_0_255, condB_wscale,
           itok_Bx4096_0_255, condB_bscale, itok_B_3_7, _lenS, L0_cond_Wq, L0_cond_Wk, L0_cond_Wv, L0_cond_Wo,
           L0_cond_q_norm_w, L0_cond_k_norm_w, L0_cond_k_cache, L0_cond_v_cache, L1_cond_weights, L2_cond_weight,
           L2_cond_bias, L3_cond_A, L3_cond_B):
    import concourse.bacc as bacc
    from concourse.bass_utils import run_bass_kernel_spmd

    def rep(a, n=P):
        return np.broadcast_to(np.asarray(a).reshape(1, -1), (n, np.asarray(a).size))

    def by_row(a):
        a = np.asarray(a).reshape(TILES, BT, 1, -1)
        return np.broadcast_to(a, (TILES, BT, S, a.shape[-1])).reshape(TILES, P, -1).transpose(1, 0, 2)

    def weights(w, heads):
        w = np.asarray(w).reshape(GROUPS, heads // GROUPS * D, KC, P)
        return w.transpose(0, 3, 2, 1)

    x, table = np.asarray(x), np.asarray(itok_Bx16_0_63)
    pages = np.broadcast_to(table.reshape(B, CH, P // PSIZE, 1), (B, CH, P // PSIZE, PSIZE)).reshape(B * CH, P).T

    def cache(c):
        return np.asarray(c).reshape(PAGES * PSIZE, GROUPS, GH * D).transpose(1, 0, 2)

    arrays = {
        **constants(),
        "tbl_rep": pages,
        "len_rep": rep(itok_B_207_1644),
        "pos_rep": by_row(itok_B_207_1644)[:, :, 0],
        "cond_rep": by_row(itok_B_0_15)[:, :, 0],
        "scale_rep": rep(condB_scale),
        "wscale_rep": rep(condB_wscale),
        "zp_rep": rep(_lenS),
        "q_norm_rep": rep(L0_cond_q_norm_w),
        "k_norm_rep": rep(L0_cond_k_norm_w),
        "x_nat": x.reshape(TILES, P, HID).transpose(1, 0, 2),
        "xT": x.reshape(TILES, P, KC, P).transpose(0, 3, 2, 1),
        "wqkv": np.concatenate([weights(L0_cond_Wq, HQ), weights(L0_cond_Wk, HK), weights(L0_cond_Wv, HK)], axis=3),
        "wo": np.asarray(L0_cond_Wo).reshape(HID, GROUPS, QH, D).transpose(1, 3, 2, 0),
        "kv": np.concatenate([cache(L0_cond_k_cache), cache(L0_cond_v_cache)], axis=2).reshape(GROUPS * PAGES * PSIZE, -1),
        "mix": np.asarray(L1_cond_weights).reshape(CONDS * S, S),
        "weightT": np.asarray(L2_cond_weight).reshape(HID, KC, P).transpose(2, 1, 0),
        "bias_rep": rep(L2_cond_bias),
        "wq": np.asarray(itok_Bx4096x4096_0_255).reshape(B, HID, KC, P).transpose(0, 3, 2, 1).reshape(B, P, KC * HID),
        "bq": np.asarray(itok_Bx4096_0_255),
        "scale_col": np.asarray(condB_scale).reshape(B, 1),
        "bscale_col": np.asarray(condB_bscale).reshape(B, 1),
        "A_all": np.asarray(L3_cond_A).transpose(0, 2, 1).reshape(NAD * RANK, HID),
        "B_all": np.asarray(L3_cond_B).reshape(NAD * RANK, KC, P).transpose(2, 1, 0),
        "aid_rep": rep(np.repeat(np.asarray(itok_B_3_7), S)),
    }
    arrays = {k: np.ascontiguousarray(a) for k, a in arrays.items()}
    nc = bacc.Bacc("TRN2", target_bir_lowering=False, num_devices=1)
    tensors = {k: nc.dram_tensor(k, a.shape, mybir.dt.from_np(a.dtype), kind="ExternalInput").ap() for k, a in arrays.items()}
    tensors["out"] = nc.dram_tensor("out", (TILES, P, HID), F32, kind="ExternalOutput").ap()
    build(nc, tensors)
    r = run_bass_kernel_spmd(nc, [arrays], core_ids=[0])
    return r.results[0]["out"].reshape(B, S, HID)
```

```python
import numpy as np
import concourse.bass as bass
from concourse import mybir
from contextlib import ExitStack

F32 = mybir.dt.float32
F32R = mybir.dt.float32r
I32 = mybir.dt.int32
BF16 = mybir.dt.bfloat16
ALU = mybir.AluOpType
ACT = mybir.ActivationFunctionType
AX = mybir.AxisListType

B, S, HID = 32, 32, 512
D, HQ, HK = 128, 32, 8
REP = HQ // HK
PAGES, PSIZE, NPP = 64, 32, 16
L = NPP * PSIZE
KEYS = L + S
P = 128
KC = HID // P
BT = P // S
TILES = B // BT
GH = 2
GROUPS = HK // GH
QH = GH * REP
ROUNDS = GROUPS * TILES
PAIRS = BT * GH
HALF = PAIRS // 2
CH = L // P
PCOLS = (CH + 1) * P
QKV = (QH + 2 * GH) * D
NORMED = QH + GH
CONDS, NAD, RANK = 16, 8, 16
HEADS = (range(0, REP), range(REP, QH), range(QH, NORMED))
SCALE = 1.0 / float(np.sqrt(D))
EPS = 1e-6
MASKED = -1e30
TWO_PI = 2.0 * np.pi
PI_1 = 6.28125
PI_2 = float(np.float32(np.round((TWO_PI - PI_1) * 2.0 ** 22) / 2.0 ** 22))
PI_3 = float(TWO_PI - PI_1 - PI_2)
WAVE = 4
WO_PARTS = 2
HALVES = 2
W_AT = ({2: (0,), 3: (1,), 7: (2,), 8: (3,)}, {2: (4, 5)})
WO_AT = {2: (0,), 3: (1,), 7: (2,), 8: (3,)}
WAVES = TILES // WAVE
TAIL_STEPS = 1 + BT + 2 + KC
ROUNDER = 1.5 * 2.0 ** 23
PI_F = 3.1415925


def constants():
    key_pos = np.concatenate([np.arange(L), np.full(S, -2.0 ** 31)]).astype(np.float32)
    inv_freq = (1.0 / np.float32(10000.0) ** (np.arange(0, D, 2, dtype=np.float32) / np.float32(D))).astype(np.float32)
    lane = np.arange(P)
    cols = np.zeros((P, 8), np.float32)
    cols[:, 0] = lane % S
    cols[:, 1] = lane // RANK
    cols[:, 2] = -0.5
    return {
        "c_ident": np.eye(P, dtype=np.float32),
        "c_key_pos": np.broadcast_to(key_pos, (P, KEYS)).copy(),
        "c_inv_freq": np.broadcast_to(inv_freq, (P, D // 2)).copy(),
        "c_cols": cols,
    }


def build(nc, t):
    ctx = ExitStack()
    with ctx:
        def sb(name, shape, dt=F32):
            return ctx.enter_context(nc.sbuf_tensor(name + "_sb", shape, dt))

        def sem(name):
            return ctx.enter_context(nc.semaphore(name))

        ident = sb("ident", [P, P])
        key_pos = sb("key_pos", [P, KEYS])
        cols = sb("cols", [P, 8])
        acc = sb("acc", [P, HID])
        w_hi = sb("w_hi", [P, KC, QKV], F32R)
        w_lo = sb("w_lo", [P, KC, QKV], F32R)
        wo_hi = sb("wo_hi", [P, QH, HID], F32R)
        wo_lo = sb("wo_lo", [P, QH, HID], F32R)
        x_in = sb("x_in", [P, KC, P])
        x_hi = sb("x_hi", [P, KC, P], F32R)
        x_lo = sb("x_lo", [P, KC, P], F32R)
        qraw = sb("qraw", [P, NORMED, D])
        rotated = sb("rotated", [P, NORMED, D])
        qrope = sb("qrope", [P, NORMED, D])
        ssq = sb("ssq", [P, NORMED])
        rstd = sb("rstd", [P, NORMED])
        varr = sb("varr", [P, NORMED])
        v_nat = sb("v_nat", [P, GH * D])
        v_new = sb("v_new", [P, BT, GH * D])
        qT = sb("qT", [P, GH, BT, REP * S])
        kT_new = sb("kT_new", [P, GH, P])
        kv = sb("kv", [P, BT, CH, 2 * GH * D])
        kT = sb("kT", [P, 2, L])
        sc = sb("sc", [P, 2, KEYS])
        bias = sb("bias", [P, 2])
        probs = sb("probs", [P, 2, PCOLS])
        sums = sb("sums", [P, PAIRS])
        inv = sb("inv", [P, PAIRS])
        pT = sb("pT", [P, 2, PCOLS])
        o_nat = sb("o_nat", [P, HALF, D])
        oT_hi = sb("oT_hi", [P, QH, BT, S], F32R)
        oT_lo = sb("oT_lo", [P, QH, BT, S], F32R)
        page_rows = sb("page_rows", [P, GROUPS, B * CH], I32)
        rows_now = sb("rows_now", [P, BT, CH], I32)
        lens = sb("lens", [P, B])
        mask = sb("mask", [P, 2, KEYS], BF16)
        rope = sb("rope", [P, 4, D])
        wT = sb("wT", [P, KC, HID])
        wq_in = sb("wq_in", [P, KC * HID], I32)
        stage = sb("stage", [P, KC * HID])
        dscale = sb("dscale", [P, B])
        small = sb("small", [P, 8, B])

        psum = ctx.enter_context(nc.psum_tensor("psum", [P, 8 * 512], F32))

        def bank(b, n=512):
            return psum[:, 512 * b:512 * b + n]

        SC, PT, KT, O, MA, MB = 0, 2, 4, 5, 6, 7

        names = """consts_in params_in big_in rows_ready tabs_in xt_in w_in w1_in w2_in vnew_in wq_loaded
            x_hi_done x_lo_done w_hi_done w_lo_done wo_hi_done wo_lo_done w_parts wo_parts ropes_made ropes_out rope_in stream_in acc_in acc_out x1_in ot_hi
            pool_waits vector_waits sync_waits kv_in0 kv_in1 kv_in2 kv_in3 kv_used0 kv_used1 kv_used2 kv_used3 zeroed
            rows_now_in0 rows_now_in1 rows_now_in2 rows_now_in3 mix_in rows_v angles
            kt_psum kt_sb s_psum s_done p_sb pt_psum pt_sb pv_done o_sb ot_psum ot_sb
            qt_psum qt_sb_a qt_sb_v kn_psum kn_sb proj_psum raw_a raw_v v_sb crossed multiplied
            sq_done rstd_done ab_done rope_add mask_done var_done
            wo_psum acc_done dw_done chain achain
            bq_psum f_x2p f_x2s f_x3p f_x3s f_x3tp f_x3ts f_bxp f_bxs f_yp f_out out_dma wdone tail_p""".split()
        s = {n: sem(n) for n in names}

        bcol = sb("bcol", [P, 8])
        cond_i = sb("cond_i", [P, TILES], I32)
        mix_rows = sb("mix_rows", [P, TILES], I32)

        w_stage = stage[:].rearrange("p (k n) -> p k n", k=KC)
        wo_stage = stage[:].rearrange("p (h n) -> p h n", h=QH // WO_PARTS)
        w_stages = [w_stage, wq_in[:].bitcast(F32).rearrange("p (k n) -> p k n", k=KC), kv[:, 1]]
        ropes = kv[:, BT // 2:BT].rearrange("p b c (f d) -> p (b c) f d", f=4)

        x2T, x3, x3T, y = (kv[:, j] for j in range(4))
        x2T = x2T.rearrange("p t (k n) -> p t k n", k=KC)
        x3T = x3T.rearrange("p t (k n) -> p t k n", k=KC)
        bx = o_nat
        x1_now = wq_in[:].bitcast(F32).rearrange("p (t n) -> p t n", t=WAVE)
        bT = qraw[:, 0:4, :]
        aT = qraw[:, 4:8, :].rearrange("p h d -> p (h d)")
        adapter = stage[:, 0:B * S]
        mix_all = stage[:, B * S:B * S + TILES * S].rearrange("p (t c) -> p t c", t=TILES)
        aid_i = adapter.bitcast(I32)
        mix = rotated[:, 0:8, :]
        bias_row = qrope[:, 0:4, :].rearrange("p h d -> p (h d)")
        bq_f = qrope[0:B, 4:8, :].rearrange("p h d -> p (h d)")
        wb = qrope[0:B, 8, :]
        bq_i = rope[0:B].rearrange("p f d -> p (f d)").bitcast(I32)

        block = ctx.enter_context(nc.Block())

        @block.sync
        def _(sp):
            sp.dma_start(cols[:], t["c_cols"]).then_inc(s["params_in"], 16)
            sp.dma_start(kT[:, 0, 0:B * CH].bitcast(I32), t["tbl_rep"]).then_inc(s["params_in"], 16)
            sp.dma_start(small[:, 0, :].bitcast(I32), t["len_rep"]).then_inc(s["params_in"], 16)
            sp.dma_start(small[:, 1, 0:TILES].bitcast(I32), t["pos_rep"]).then_inc(s["params_in"], 16)
            sp.dma_start(cond_i[:], t["cond_rep"]).then_inc(s["params_in"], 16)
            sp.dma_start(sc[:, 0, 0:D // 2], t["c_inv_freq"]).then_inc(s["params_in"], 16)
            sp.dma_start(sc[:, 0, D:2 * D], t["q_norm_rep"]).then_inc(s["params_in"], 16)
            sp.dma_start(sc[:, 0, 2 * D:3 * D], t["k_norm_rep"]).then_inc(s["params_in"], 16)
            sp.dma_start(x_in[:], t["xT"][0]).then_inc(s["xt_in"], 16)
            for part in range(3):
                cs = slice(512 * part, 512 * (part + 1))
                sp.dma_start(w_stages[part], t["wqkv"][0][:, :, cs]).then_inc(s[("w_in", "w1_in", "w2_in")[part]], 16)
            sp.dma_start(ident[:], t["c_ident"]).then_inc(s["consts_in"], 16)
            sp.dma_start(key_pos[:], t["c_key_pos"]).then_inc(s["big_in"], 16)
            sp.dma_start(small[:, 2, :], t["scale_rep"]).then_inc(s["big_in"], 16)
            sp.dma_start(small[:, 3, :], t["wscale_rep"]).then_inc(s["big_in"], 16)
            sp.dma_start(small[:, 4, :].bitcast(I32), t["zp_rep"]).then_inc(s["big_in"], 16)
            sp.dma_start(wT[:], t["weightT"]).then_inc(s["big_in"], 16)
            sp.dma_start(t["stream"], t["x_nat"]).then_inc(s["stream_in"], 16)
            sp.wait_ge(s["ropes_made"], 1)
            sp.dma_start(t["ropes"], ropes.rearrange("p t f d -> p (t f d)")).then_inc(s["ropes_out"], 16)
            sp.wait_ge(s["zeroed"], 2)

            def load_round(m, i, store=True, load=True, landing=()):
                sp.wait_ge(s["x_lo_done"], m)
                sp.sem_inc(s["sync_waits"], 1)
                sp.dma_start(x_in[:], t["xT"][bass.ds(i, 1)].rearrange("a p k n -> p (a k) n")).then_inc(s["xt_in"], 16)
                if store:
                    store_stream(m - 3, i + (TILES - 3))
                if load:
                    load_stream(m - 2, i + (TILES - 2))
                load_deltas(m - 1)
                for load_part, g, part in landing:
                    load_part(g, part)
                sp.wait_ge(s["multiplied"], 3 * m)
                sp.sem_inc(s["sync_waits"], 1)
                sp.dma_start(rope[:].rearrange("p f d -> p (f d)"), t["ropes"][:, bass.ds(i * (4 * D), 4 * D)]).then_inc(s["rope_in"], 16)
                load_values(m - 1)

            def load_weights(g, part):
                sp.wait_ge(s["w_lo_done"], g * (3 * HALVES) + part * HALVES)
                sp.sem_inc(s["sync_waits"], 1)
                if part == 0:
                    sp.wait_ge(s["wo_lo_done"], g * (WO_PARTS * HALVES))
                    sp.sem_inc(s["sync_waits"], 1)
                sp.dma_start(w_stage, t["wqkv"][bass.ds(g, 1), :, :, 512 * part:512 * (part + 1)].rearrange("a p k n -> p (a k) n")
                             ).then_inc(s["w_parts"], 16)

            def load_output_weights(g, part):
                sp.wait_ge(s["w_lo_done"], g * (3 * HALVES) + 3 * HALVES)
                sp.sem_inc(s["sync_waits"], 1)
                if part:
                    sp.wait_ge(s["wo_lo_done"], g * (WO_PARTS * HALVES) + part * HALVES)
                    sp.sem_inc(s["sync_waits"], 1)
                hs = slice(QH // WO_PARTS * part, QH // WO_PARTS * (part + 1))
                sp.dma_start(wo_stage, t["wo"][bass.ds(g, 1), :, hs, :].rearrange("a p h n -> p (a h) n")).then_inc(s["wo_parts"], 16)

            def store_stream(n, i):
                sp.wait_ge(s["acc_done"], n + 1)
                sp.sem_inc(s["sync_waits"], 1)
                sp.dma_start(t["stream"][bass.ds(i % TILES, 1)].rearrange("a p n -> (a p) n"), acc[:]).then_inc(s["acc_out"], 16)

            def load_stream(n, i, first=False):
                if not first:
                    sp.wait_ge(s["acc_out"], n * 16)
                    sp.sem_inc(s["sync_waits"], 1)
                sp.dma_start(acc[:], t["stream"][bass.ds(i % TILES, 1)].rearrange("a p n -> (a p) n")).then_inc(s["acc_in"], 16)

            def load_deltas(m):
                if not (isinstance(m, int) and m == 0):
                    sp.wait_ge(s["dw_done"], m)
                    sp.sem_inc(s["sync_waits"], 1)
                else:
                    sp.wait_ge(s["w_lo_done"], 2 * HALVES)
                sp.dma_start(wq_in[:], t["wq"][bass.ds(m, 1)].rearrange("a p n -> (a p) n")).then_inc(s["wq_loaded"], 16)

            def load_values(m):
                sp.wait_ge(s["v_sb"], m + 1)
                sp.sem_inc(s["sync_waits"], 1)
                if not (isinstance(m, int) and m == 0):
                    sp.wait_ge(s["pv_done"], m * PAIRS)
                    sp.sem_inc(s["sync_waits"], 1)
                for b in range(BT):
                    sp.dma_start(v_new[0:S, b, :], v_nat[S * b:S * (b + 1), :]).then_inc(s["vnew_in"], 16)

            sp.wait_ge(s["ropes_out"], 16)
            load_output_weights(0, 0)
            load_round(1, 1, store=False, load=False)
            sp.wait_ge(s["stream_in"], 16)
            load_stream(0, 0, True)
            load_round(2, 2, store=False, load=False, landing=((load_output_weights, 0, 1),))
            with sp.Fori(3, TILES) as i:
                load_round(i, i)
            with sp.Fori(1, GROUPS) as g:
                load_weights(g, 0)
                load_round(g * TILES, 0, landing=((load_weights, g, 1), (load_weights, g, 2)))
                load_round(g * TILES + 1, 1, landing=((load_output_weights, g, 0),))
                load_round(g * TILES + 2, 2, landing=((load_output_weights, g, 1),))
                with sp.Fori(3, TILES) as i:
                    load_round(g * TILES + i, i)
            store_stream(ROUNDS - 3, ROUNDS - 3)
            load_stream(ROUNDS - 2, ROUNDS - 2)
            load_deltas(ROUNDS - 1)
            load_values(ROUNDS - 1)
            sp.wait_ge(s["kn_psum"], ROUNDS)
            sp.dma_start(bT, t["B_all"]).then_inc(s["tabs_in"], 16)
            sp.dma_start(aT, t["A_all"]).then_inc(s["tabs_in"], 16)
            sp.dma_start(aid_i, t["aid_rep"]).then_inc(s["tabs_in"], 16)
            sp.dma_start(bq_i, t["bq"]).then_inc(s["tabs_in"], 16)
            sp.dma_start(bcol[0:B, 0:1], t["scale_col"]).then_inc(s["tabs_in"], 16)
            sp.dma_start(bcol[0:B, 1:2], t["bscale_col"]).then_inc(s["tabs_in"], 16)
            sp.dma_start(bias_row, t["bias_rep"]).then_inc(s["tabs_in"], 16)
            sp.wait_ge(s["dw_done"], ROUNDS)
            sp.dma_start(x1_now, t["stream"][0:WAVE].rearrange("t p n -> p t n")).then_inc(s["x1_in"], 16)
            store_stream(ROUNDS - 2, ROUNDS - 2)
            load_stream(ROUNDS - 1, ROUNDS - 1)
            store_stream(ROUNDS - 1, ROUNDS - 1)
            sp.wait_ge(s["acc_out"], 16 * ROUNDS)
            sp.wait_ge(s["f_x2p"], WAVE)
            sp.dma_start(x1_now, t["stream"][WAVE:2 * WAVE].rearrange("t p n -> p t n")).then_inc(s["x1_in"], 16)
            with sp.Fori(0, WAVES) as w:
                for j in range(WAVE):
                    sp.wait_ge(s["f_out"], w * WAVE + (j + 1))
                    sp.sem_inc(s["sync_waits"], 1)
                    sp.dma_start(t["out"][bass.ds(w * WAVE + j, 1)].rearrange("a p n -> (a p) n"), y[:, j, :]).then_inc(s["out_dma"], 16)
            sp.wait_ge(s["out_dma"], 16 * TILES)

        @block.gpsimd
        def _(po):
            po.memset(probs[:], 0.0).then_inc(s["zeroed"], 1)
            po.memset(v_new[:], 0.0).then_inc(s["zeroed"], 1)
            po.wait_ge(s["rows_ready"], 1)
            rows = page_rows[:].rearrange("p g c -> p (g c)")

            def inverse_root(m1):
                po.wait_ge(s["sq_done"], 3 * m1)
                po.sem_inc(s["pool_waits"], 1)
                po.tensor_scalar(varr[:], ssq[:], 1.0 / D, EPS, ALU.mult, ALU.add).then_inc(s["var_done"], 1)
                po.wait_ge(s["var_done"], m1)
                po.sem_inc(s["pool_waits"], 1)
                po.tensor_tensor(rstd[:], varr[:], cols[:, 2:3].to_broadcast([P, NORMED]), ALU.pow).then_inc(s["rstd_done"], 1)

            def gather(n, first=False):
                for b in range(BT):
                    if first:
                        if b == 1:
                            for part in range(3):
                                cs = slice(512 * part, 512 * (part + 1))
                                po.wait_ge(s["w_hi_done"], (part + 1) * HALVES)
                                po.tensor_tensor(w_lo[:, :, cs], w_stages[part], w_hi[:, :, cs].bitcast(F32),
                                                 ALU.subtract).then_inc(s["w_lo_done"], HALVES)
                            po.wait_ge(s["w_lo_done"], 3 * HALVES)
                        elif b == 2:
                            inverse_root(1)
                            po.wait_ge(s["ropes_out"], 16)
                            po.wait_ge(s["multiplied"], 3)
                    else:
                        po.wait_ge(s[f"kv_used{b}"], n - 1)
                        po.sem_inc(s["pool_waits"], 1)
                    po.tensor_copy(rows_now[:, b, :], rows[:, bass.ds((n - 1) * (BT * CH) + b * CH, CH)]
                                   ).then_inc(s[f"rows_now_in{b}"], 1)
                    po.wait_ge(s[f"rows_now_in{b}"], n)
                    po.sem_inc(s["pool_waits"], 1)
                    for c in range(CH):
                        po.indirect_dma_start(out=kv[:, b, c, :], out_offset=None, in_=t["kv"],
                                              in_offset=bass.IndirectOffsetOnAxis(ap=rows_now[:, b, c:c + 1], axis=0)
                                              ).then_inc(s[f"kv_in{b}"], 16)

            gather(1, True)
            inverse_root(2)
            with po.Fori(2, ROUNDS) as n:
                gather(n)
                inverse_root(n + 1)
            gather(ROUNDS)
            po.wait_ge(s["wo_lo_done"], WO_PARTS * HALVES * GROUPS)
            for i in range(TILES):
                po.indirect_dma_start(out=mix_all[:, i, :], out_offset=None, in_=t["mix"],
                                      in_offset=bass.IndirectOffsetOnAxis(ap=mix_rows[:, i:i + 1], axis=0)
                                      ).then_inc(s["mix_in"], 16)

        @block.scalar
        def _(act):
            def split_tokens(m):
                act.wait_ge(s["xt_in"], 16 * (m + 1))
                if not (isinstance(m, int) and m == 0):
                    act.wait_ge(s["proj_psum"], 3 * m)
                nc.scalar.copy(x_hi[:], x_in[:]).then_inc(s["x_hi_done"], 1)

            def split_weights(piece):
                src = 256 * (piece % HALVES)
                nc.scalar.copy(w_hi[:, :, 256 * piece:256 * (piece + 1)], w_stage[:, :, src:src + 256]).then_inc(s["w_hi_done"], 1)

            def split_output_weights(piece):
                src = 2 * (piece % HALVES)
                nc.scalar.copy(wo_hi[:, 2 * piece:2 * (piece + 1), :], wo_stage[:, src:src + 2, :]).then_inc(s["wo_hi_done"], 1)

            split_tokens(0)
            for part, landed in enumerate(("w_in", "w1_in", "w2_in")):
                act.wait_ge(s[landed], 16)
                nc.scalar.copy(w_hi[:, :, 512 * part:512 * (part + 1)], w_stages[part]).then_inc(s["w_hi_done"], HALVES)
            sin_t = qrope[:, 0:4, :].rearrange("p h d -> p (h d)")
            cos_t = qrope[:, 4:8, :].rearrange("p h d -> p (h d)")
            act.wait_ge(s["angles"], 1)
            nc.scalar.activation(sin_t, sin_t, ACT.Sin)
            nc.scalar.activation(cos_t, cos_t, ACT.Sin).then_inc(s["achain"], 1)

            def take_proj(m, first=False):
                act.wait_ge(s["proj_psum"], 3 * m + 1)
                if not first:
                    act.wait_ge(s["rope_add"], 3 * m)
                nc.scalar.copy(qraw[:, 0:REP, :].rearrange("p h d -> p (h d)"), bank(MA)).then_inc(s["raw_a"], 1)

            def take_kv(m, first=False):
                act.wait_ge(s["proj_psum"], 3 * m + 3)
                nc.scalar.copy(qraw[:, QH:NORMED, :].rearrange("p h d -> p (h d)"), bank(MA, GH * D)).then_inc(s["raw_a"], 1)
                if not first:
                    act.wait_ge(s["vnew_in"], m * (16 * BT))
                nc.scalar.copy(v_nat[:], psum[:, 512 * MA + GH * D:512 * (MA + 1)]).then_inc(s["v_sb"], 1)

            def squares(m, piece):
                if piece == 0:
                    act.wait_ge(s["raw_a"], 2 * m + 1)
                    act.wait_ge(s["rstd_done"], m)
                elif piece == 1:
                    act.wait_ge(s["raw_v"], m + 1)
                else:
                    act.wait_ge(s["raw_a"], 2 * m + 2)
                for h in HEADS[piece]:
                    ins = nc.scalar.activation(qrope[:, h, :], qraw[:, h, :], ACT.Square, accum_out=ssq[:, h:h + 1])
                ins.then_inc(s["sq_done"], 1)

            def take_queries(n):
                act.wait_ge(s["qt_psum"], 2 * n + 1)
                nc.scalar.copy(qT[:, 0].rearrange("p b (j s) -> p j b s", j=REP),
                               bank(MA).rearrange("p (j b s) -> p j b s", j=REP, b=BT)).then_inc(s["qt_sb_a"], 1)

            def take_new_keys(n):
                act.wait_ge(s["kn_psum"], n + 1)
                nc.scalar.copy(kT_new[:].rearrange("p h k -> p (h k)"), bank(MA, GH * P)).then_inc(s["kn_sb"], 1)

            def keys(n, i):
                act.wait_ge(s["kt_psum"], n * PAIRS + (i + 1))
                nc.scalar.copy(kT[:, i % 2, :], bank(KT)).then_inc(s["kt_sb"], 1)

            take_proj(0, True)
            act.wait_ge(s["ropes_made"], 1)
            squares(0, 0)
            squares(0, 1)
            take_kv(0, True)
            squares(0, 2)
            take_queries(0)
            keys(0, 0)
            take_new_keys(0)

            def round_(n, last=False, new=None, weights={}, output_weights={}):
                for i in range(PAIRS + 2):
                    if i + 1 < PAIRS:
                        keys(n, i + 1)
                    if 1 <= i <= PAIRS:
                        j = i - 1
                        act.wait_ge(s["pv_done"], n * PAIRS + max(0, j - 1))
                        act.wait_ge(s["pt_psum"], n * PAIRS + (j + 1))
                        nc.scalar.copy(pT[:, j % 2, :], psum[:, 512 * PT:512 * PT + PCOLS]).then_inc(s["pt_sb"], 1)
                    if i < PAIRS:
                        act.wait_ge(s["s_done"], n * PAIRS + (i + 1))
                        act.wait_ge(s["pt_psum"], n * PAIRS + (i - 1 if i >= 2 else 0))
                        nc.scalar.activation(probs[:, i % 2, 0:KEYS], sc[:, i % 2, :], ACT.Exp, bias=bias[:, i % 2:i % 2 + 1],
                                             scale=-1.0, accum_out=sums[:, i:i + 1]).then_inc(s["p_sb"], 1)
                    if i == 0 and not last:
                        split_tokens(n + 1)
                    for piece in weights.get(i, ()):
                        act.wait_ge(s["w_parts"], (new - 1) * 48 + 16 * (piece // HALVES + 1))
                        split_weights(piece)
                    for piece in output_weights.get(i, ()):
                        act.wait_ge(s["wo_parts"], new * (16 * WO_PARTS) + 16 * (piece // HALVES + 1))
                        split_output_weights(piece)
                    if i == 1 and not last:
                        take_proj(n + 1)
                    if i == 3 and not last:
                        take_kv(n + 1)
                    if i in (2, 3, 4) and not last:
                        squares(n + 1, i - 2)
                    if i == 6:
                        take_outputs(n, 0)
                if not last:
                    take_queries(n + 1)
                    keys(n + 1, 0)
                    take_new_keys(n + 1)
                take_outputs(n, 1)

            def take_outputs(n, half):
                act.wait_ge(s["ot_psum"], 2 * n + (half + 1))
                nb = BT // 2
                nc.scalar.copy(oT_hi[:, :, nb * half:nb * (half + 1), :].rearrange("p h b s -> p b h s"),
                               bank(MB).rearrange("p (b h s) -> p b h s", b=nb, h=QH)).then_inc(s["ot_hi"], 1)

            round_(0, new=0, output_weights=WO_AT)
            with act.Fori(0, GROUPS - 1) as g:
                with act.Fori(1, TILES - 2) as i:
                    round_(g * TILES + i)
                round_(g * TILES + (TILES - 2), new=g + 1, weights=W_AT[0])
                round_(g * TILES + (TILES - 1), new=g + 1, weights=W_AT[1])
                round_(g * TILES + TILES, new=g + 1, output_weights=WO_AT)
            with act.Fori(ROUNDS - TILES + 1, ROUNDS - 1) as n:
                round_(n)
            round_(ROUNDS - 1, last=True)

            act.wait_ge(s["pv_done"], ROUNDS * PAIRS)
            with act.Fori(0, WAVES) as w:
                for j in range(WAVE):
                    act.wait_ge(s["f_x2p"], w * WAVE + (j + 1))
                    nc.scalar.copy(x2T[:, j].rearrange("p k n -> p (k n)"), bank(j % 2)).then_inc(s["f_x2s"], 1)
                for j in range(WAVE):
                    act.wait_ge(s["f_x3tp"], w * WAVE + (j + 1))
                    nc.scalar.copy(x3T[:, j].rearrange("p k n -> p (k n)"), bank(4 + j % 2)).then_inc(s["f_x3ts"], 1)

        @block.vector
        def _(v):
            link = [0]

            def chained(ins):
                link[0] += 1
                ins.then_inc(s["chain"], 1)
                v.wait_ge(s["chain"], link[0])

            v.wait_ge(s["params_in"], 16 * 8)
            tbl = kT[:, 0, 0:B * CH].bitcast(I32)
            row_f = kT[:, 1, 0:B * CH]
            chained(nc.vector.tensor_scalar(row_f, tbl, float(PSIZE), cols[:, 0:1], ALU.mult, ALU.add))
            for g in range(GROUPS):
                chained(nc.vector.tensor_scalar(page_rows[:, g, :], row_f, float(g * PAGES * PSIZE), None, ALU.add))
            chained(nc.vector.tensor_copy(small[:, 5, 0:TILES], cond_i[:]))
            chained(nc.vector.tensor_scalar(mix_rows[:], small[:, 5, 0:TILES], float(S), cols[:, 0:1], ALU.mult, ALU.add))
            nc.vector.tensor_copy(lens[:], small[:, 0, :].bitcast(I32)).then_inc(s["rows_ready"], 1)
            v.wait_ge(s["rows_ready"], 1)
            def split_tokens(m):
                v.wait_ge(s["x_hi_done"], m + 1)
                nc.vector.tensor_tensor(x_lo[:], x_in[:], x_hi[:].bitcast(F32), ALU.subtract).then_inc(s["x_lo_done"], 1)

            def split_weights(piece):
                cs, src = slice(256 * piece, 256 * (piece + 1)), 256 * (piece % HALVES)
                nc.vector.tensor_tensor(w_lo[:, :, cs], w_stage[:, :, src:src + 256], w_hi[:, :, cs].bitcast(F32),
                                        ALU.subtract).then_inc(s["w_lo_done"], 1)

            def split_output_weights(piece):
                hs, src = slice(2 * piece, 2 * (piece + 1)), 2 * (piece % HALVES)
                nc.vector.tensor_tensor(wo_lo[:, hs, :], wo_stage[:, src:src + 2, :], wo_hi[:, hs, :].bitcast(F32),
                                        ALU.subtract).then_inc(s["wo_lo_done"], 1)

            pos_i = small[:, 1, 0:TILES].bitcast(I32)
            chained(nc.vector.tensor_copy(small[:, 5, 0:TILES], pos_i))
            chained(nc.vector.tensor_scalar(small[:, 6, 0:TILES], small[:, 5, 0:TILES], cols[:, 0:1], None, ALU.add))
            HD = D // 2
            ang = rotated[:, 0:4, :].rearrange("p h d -> p (h d)")
            turns = rotated[:, 4:8, :].rearrange("p h d -> p (h d)")
            for i in range(TILES):
                chained(nc.vector.tensor_scalar(ang[:, HD * i:HD * (i + 1)], sc[:, 0, 0:HD], small[:, 6, i:i + 1], None, ALU.mult))
            split_tokens(0)
            for quarter, dst in ((0.0, qrope[:, 0:4, :]), (0.25, qrope[:, 4:8, :])):
                r = dst.rearrange("p h d -> p (h d)")
                chained(nc.vector.tensor_scalar(turns, ang, 1.0 / TWO_PI, quarter, ALU.mult, ALU.add))
                chained(nc.vector.tensor_scalar(turns, turns, ROUNDER, None, ALU.add))
                chained(nc.vector.tensor_scalar(turns, turns, -ROUNDER, None, ALU.add))
                chained(nc.vector.scalar_tensor_tensor(r, turns, -PI_1, ang, ALU.mult, ALU.add))
                chained(nc.vector.scalar_tensor_tensor(r, turns, -PI_2, r, ALU.mult, ALU.add))
                chained(nc.vector.scalar_tensor_tensor(r, turns, -PI_3, r, ALU.mult, ALU.add))
                if quarter:
                    chained(nc.vector.tensor_scalar(r, r, TWO_PI / 4, None, ALU.add))
                ins = nc.vector.tensor_scalar(r, r, PI_F, -PI_F, ALU.min, ALU.max)
                if not quarter:
                    chained(ins)
            ins.then_inc(s["angles"], 1)

            v.wait_ge(s["achain"], 1)
            sin_t = qrope[:, 0:4, :].rearrange("p h d -> p (h d)").rearrange("p (t d) -> p t d", t=TILES)
            cos_t = qrope[:, 4:8, :].rearrange("p h d -> p (h d)").rearrange("p (t d) -> p t d", t=TILES)
            for kind in range(2):
                w1 = sc[:, 0, D * (1 + kind):D * (1 + kind) + HD].unsqueeze(1).to_broadcast([P, TILES, HD])
                w2 = sc[:, 0, D * (1 + kind) + HD:D * (2 + kind)].unsqueeze(1).to_broadcast([P, TILES, HD])
                chained(nc.vector.tensor_tensor(ropes[:, :, kind, 0:HD], cos_t, w1, ALU.mult))
                chained(nc.vector.tensor_tensor(ropes[:, :, kind, HD:D], cos_t, w2, ALU.mult))
                chained(nc.vector.scalar_tensor_tensor(ropes[:, :, 2 + kind, 0:HD], sin_t, -1.0, w2, ALU.mult, ALU.mult))
                last_factors = nc.vector.tensor_tensor(ropes[:, :, 2 + kind, HD:D], sin_t, w1, ALU.mult)
                if kind == 0:
                    chained(last_factors)
            last_factors.then_inc(s["ropes_made"], 1)
            v.wait_ge(s["ropes_made"], 1)

            def delta_scales():
                v.wait_ge(s["big_in"], 16 * 5)
                chained(nc.vector.tensor_tensor(dscale[:], small[:, 2, :], small[:, 3, :], ALU.mult))
                chained(nc.vector.tensor_copy(small[:, 5, :], small[:, 4, :].bitcast(I32)))
                chained(nc.vector.tensor_tensor(small[:, 6, :], small[:, 5, :], small[:, 2, :], ALU.mult))
                chained(nc.vector.tensor_reduce(small[:, 7, 0:1], small[:, 6, :], AX.X, ALU.add))
                chained(nc.vector.tensor_scalar(wT[:], wT[:], small[:, 7, 0:1], None, ALU.add))

            def take_proj(m, first=False):
                v.wait_ge(s["proj_psum"], 3 * m + 2)
                if not first:
                    v.wait_ge(s["rope_add"], 3 * m)
                nc.vector.tensor_copy(qraw[:, REP:QH, :].rearrange("p h d -> p (h d)"), bank(MB)).then_inc(s["raw_v"], 1)

            def cross(m, piece, factors):
                if piece == 0:
                    v.wait_ge(s["ab_done"], m)
                    if factors is rope:
                        v.wait_ge(s["rope_in"], 16 * m)
                    v.wait_ge(s["raw_a"], 2 * m + 1)
                elif piece == 1:
                    v.wait_ge(s["raw_v"], m + 1)
                else:
                    v.wait_ge(s["raw_a"], 2 * m + 2)
                lo, hi, kind = HEADS[piece].start, HEADS[piece].stop, piece // 2
                for half in range(2):
                    other = 1 - half
                    sn = factors[:, 2 + kind, HD * half:HD * (half + 1)].unsqueeze(1).to_broadcast([P, hi - lo, HD])
                    ins = nc.vector.tensor_tensor(rotated[:, lo:hi, HD * half:HD * (half + 1)],
                                                  qraw[:, lo:hi, HD * other:HD * (other + 1)], sn, ALU.mult)
                ins.then_inc(s["crossed"], 1)

            def multiply(m, piece, factors):
                v.wait_ge(s["sq_done"], 3 * m + (piece + 1))
                v.wait_ge(s["crossed"], 3 * m + (piece + 1))
                lo, hi, kind = HEADS[piece].start, HEADS[piece].stop, piece // 2
                c = factors[:, kind, :].unsqueeze(1).to_broadcast([P, hi - lo, D])
                nc.vector.tensor_tensor(qraw[:, lo:hi, :], qraw[:, lo:hi, :], c, ALU.mult).then_inc(s["multiplied"], 1)

            def add(m, piece):
                v.wait_ge(s["multiplied"], 3 * m + (piece + 1))
                lo, hi = HEADS[piece].start, HEADS[piece].stop
                nc.vector.tensor_tensor(rotated[:, lo:hi, :], rotated[:, lo:hi, :], qraw[:, lo:hi, :], ALU.add).then_inc(s["rope_add"], 1)

            def normalise(m):
                v.wait_ge(s["rstd_done"], m + 1)
                v.wait_ge(s["rope_add"], 3 * (m + 1))
                v.wait_ge(s["kn_psum"], m)
                nc.vector.tensor_tensor(qrope[:], rotated[:], rstd[:].unsqueeze(2).to_broadcast([P, NORMED, D]),
                                        ALU.mult).then_inc(s["ab_done"], 1)

            def take_queries(n):
                v.wait_ge(s["qt_psum"], 2 * n + 2)
                nc.vector.tensor_copy(qT[:, 1].rearrange("p b (j s) -> p j b s", j=REP),
                                      bank(MB).rearrange("p (j b s) -> p j b s", j=REP, b=BT)).then_inc(s["qt_sb_v"], 1)

            def set_mask(b, batch):
                nc.vector.tensor_scalar(mask[:, b % 2, :], key_pos[:], lens[:, batch], MASKED, ALU.is_ge, ALU.mult).then_inc(s["mask_done"], 1)

            take_proj(0, True)
            for piece in range(3):
                cross(0, piece, ropes[:, 0])
                multiply(0, piece, ropes[:, 0])
                add(0, piece)
            v.wait_ge(s["big_in"], 16 * 5)
            for b in range(2):
                set_mask(b, slice(b, b + 1))
            normalise(0)
            take_queries(0)

            def add_output(n):
                v.wait_ge(s["wo_psum"], n + 1)
                v.wait_ge(s["acc_in"], 16 * (n + 1))
                nc.vector.tensor_tensor(acc[:], bank(MB), acc[:], ALU.add).then_inc(s["acc_done"], 1)

            def round_(n, last=False, first=False, new=None, weights={}, output_weights={}):
                for i in range(PAIRS + 2):
                    if i < PAIRS:
                        if i % GH == 0:
                            v.wait_ge(s["mask_done"], n * BT + (i // GH + 1))
                        if i >= 2:
                            v.wait_ge(s["p_sb"], n * PAIRS + (i - 1))
                        else:
                            v.wait_ge(s["p_sb"], n * PAIRS)
                        v.wait_ge(s["s_psum"], n * PAIRS + (i + 1))
                        v.sem_inc(s["vector_waits"], 1)
                        nc.vector.tensor_tensor_reduce(out=sc[:, i % 2, :], in0=psum[:, 512 * SC:512 * SC + KEYS],
                                                       in1=mask[:, i // GH % 2, :], scale=-SCALE, scalar=3e38,
                                                       op0=ALU.add, op1=ALU.min,
                                                       accum_out=bias[:, i % 2:i % 2 + 1]).then_inc(s["s_done"], 1)
                    if i >= 2 and i % GH == 0:
                        b = i // GH + 1
                        v.wait_ge(s["s_done"], n * PAIRS + i)
                        if b < BT:
                            set_mask(b, bass.ds(n % TILES * BT + b, 1))
                        elif not last:
                            set_mask(b - BT, bass.ds((n + 1) % TILES * BT + (b - BT), 1))
                    if i == 0:
                        if not last:
                            split_tokens(n + 1)
                        if not first:
                            add_output(n - 1)
                    if i == 1:
                        if first:
                            delta_scales()
                        else:
                            v.wait_ge(s["dw_done"], n)
                        v.wait_ge(s["wq_loaded"], 16 * (n + 1))
                        wflat = wT[:].rearrange("p k n -> p (k n)")
                        nc.vector.scalar_tensor_tensor(wflat, wq_in[:], dscale[:, bass.ds(n, 1)], wflat, ALU.mult, ALU.add).then_inc(s["dw_done"], 1)

                    if i == 7:
                        low_outputs(n, 0)
                    for piece in weights.get(i, ()):
                        v.wait_ge(s["w_hi_done"], new * (3 * HALVES) + (piece + 1))
                        split_weights(piece)
                    for piece in output_weights.get(i, ()):
                        v.wait_ge(s["wo_hi_done"], new * (WO_PARTS * HALVES) + (piece + 1))
                        split_output_weights(piece)
                    if i == 2 and not last:
                        cross(n + 1, 0, rope)
                    if i == 3 and not last:
                        take_proj(n + 1)
                        cross(n + 1, 1, rope)
                        multiply(n + 1, 0, rope)
                        add(n + 1, 0)
                    if i == 4 and not last:
                        multiply(n + 1, 1, rope)
                        add(n + 1, 1)
                    if i == 5 and not last:
                        cross(n + 1, 2, rope)
                        multiply(n + 1, 2, rope)
                        add(n + 1, 2)
                    if i == 5:
                        outputs(n, 0)
                    if i == 6 and not last:
                        normalise(n + 1)
                    if i == 3 and last:
                        prepare_mixes()
                    if i == 4 and last:
                        prepare_bias()
                if not last:
                    take_queries(n + 1)
                outputs(n, 1)
                low_outputs(n, 1)

            def low_outputs(n, half):
                v.wait_ge(s["ot_hi"], 2 * n + (half + 1))
                nb = BT // 2
                bs = slice(nb * half, nb * (half + 1))
                nc.vector.tensor_tensor(oT_lo[:, :, bs, :].rearrange("p h b s -> p b h s"),
                                        bank(MB).rearrange("p (b h s) -> p b h s", b=nb, h=QH),
                                        oT_hi[:, :, bs, :].bitcast(F32).rearrange("p h b s -> p b h s"),
                                        ALU.subtract).then_inc(s["ot_sb"], 1)

            def outputs(n, half):
                v.wait_ge(s["p_sb"], n * PAIRS + HALF * (half + 1))
                nc.vector.reciprocal(inv[:, HALF * half:HALF * (half + 1)], sums[:, HALF * half:HALF * (half + 1)]).then_inc(s["rows_v"], 1)
                v.wait_ge(s["rows_v"], 2 * n + (half + 1))
                v.wait_ge(s["pv_done"], n * PAIRS + HALF * (half + 1))
                nc.vector.tensor_tensor(o_nat[:], bank(O).rearrange("p (i d) -> p i d", i=HALF),
                                        inv[:, HALF * half:HALF * (half + 1)].unsqueeze(2).to_broadcast([P, HALF, D]),
                                        ALU.mult).then_inc(s["o_sb"], 1)

            prepared = [0]

            def prepare(ins):
                prepared[0] += 1
                ins.then_inc(s["tail_p"], 1)
                v.wait_ge(s["tail_p"], prepared[0])

            def prepare_mixes():
                v.wait_ge(s["ab_done"], ROUNDS)
                v.wait_ge(s["mix_in"], 16 * TILES)
                prepare(nc.vector.tensor_copy(mix, ident[:].unsqueeze(1).to_broadcast([P, TILES, P])))
                for b in range(BT):
                    r = slice(S * b, S * (b + 1))
                    prepare(nc.vector.tensor_tensor(mix[r, :, S * b:S * (b + 1)], mix_all[r],
                                                    ident[r, S * b:S * (b + 1)].unsqueeze(1).to_broadcast([S, TILES, S]), ALU.add))

            def prepare_bias():
                v.wait_ge(s["tabs_in"], 16 * 7)
                prepare(nc.vector.tensor_copy(bq_f, bq_i))
                prepare(nc.vector.tensor_tensor(bcol[0:B, 3:4], bcol[0:B, 0:1], bcol[0:B, 1:2], ALU.mult))
                nc.vector.tensor_copy(wb, bcol[0:B, 3:4].to_broadcast([B, P])).then_inc(s["wdone"], 1)

            round_(0, new=0, output_weights=WO_AT, first=True)
            with v.Fori(0, GROUPS - 1) as g:
                with v.Fori(1, TILES - 2) as i:
                    round_(g * TILES + i)
                round_(g * TILES + (TILES - 2), new=g + 1, weights=W_AT[0])
                round_(g * TILES + (TILES - 1), new=g + 1, weights=W_AT[1])
                round_(g * TILES + TILES, new=g + 1, output_weights=WO_AT)
            with v.Fori(ROUNDS - TILES + 1, ROUNDS - 1) as n:
                round_(n)
            round_(ROUNDS - 1, last=True)

            for k in range(KC):
                prepare(nc.vector.tensor_tensor(wT[:, k, P * k:P * (k + 1)], wT[:, k, P * k:P * (k + 1)], ident[:], ALU.add))
            prepare(nc.vector.tensor_scalar(bias_row, bias_row, small[:, 7, 0:1], None, ALU.add))
            add_output(ROUNDS - 1)
            v.wait_ge(s["bq_psum"], 1)
            prepare(nc.vector.tensor_tensor(bias_row, bank(5), bias_row, ALU.add))
            prepare(nc.vector.tensor_copy(adapter, aid_i))
            prepare(nc.vector.tensor_scalar(adapter, adapter, cols[:, 1:2], None, ALU.is_equal))
            with v.Fori(0, WAVES) as w:
                for j in range(WAVE):
                    v.wait_ge(s["f_x3p"], w * WAVE + (j + 1))
                    nc.vector.tensor_tensor(x3[:, j, :], bank(2 + j % 2), bias_row, ALU.add).then_inc(s["f_x3s"], 1)
                v.wait_ge(s["f_bxp"], w + 1)
                nc.vector.tensor_tensor(bx.rearrange("p t n -> p (t n)"), bank(6), adapter[:, bass.ds(w * (WAVE * P), WAVE * P)],
                                        ALU.mult).then_inc(s["f_bxs"], 1)
                v.wait_ge(s["f_x3s"], (w + 1) * WAVE)
                v.wait_ge(s["out_dma"], w * (16 * WAVE))
                for j in range(WAVE):
                    v.wait_ge(s["f_yp"], w * WAVE + (j + 1))
                    nc.vector.tensor_tensor(y[:, j, :], bank(7 - j % 2), x3[:, j, :], ALU.add).then_inc(s["f_out"], 1)

        @block.tensor
        def _(pe):
            mm = nc.tensor.matmul

            def project(m, part, first=False, second=False):
                pe.wait_ge(s["w_lo_done"], m // TILES * (3 * HALVES) + (part + 1) * HALVES)
                if part == 0:
                    pe.wait_ge(s["x_lo_done"], m + 1)
                elif part == 1:
                    if not (first or second):
                        pe.wait_ge(s["acc_done"], m - 1)
                else:
                    pe.wait_ge(s["raw_a"], 2 * m + 1)
                out, cs = bank(MB if part == 1 else MA), slice(512 * part, 512 * (part + 1))
                for k in range(KC):
                    mm(out, x_hi[:, k, :], w_hi[:, k, cs], start=(k == 0), stop=False)
                    mm(out, x_hi[:, k, :], w_lo[:, k, cs], start=False, stop=False)
                    ins = mm(out, x_lo[:, k, :], w_hi[:, k, cs], start=False, stop=(k == KC - 1))
                ins.then_inc(s["proj_psum"], 1)

            def keys(n, i):
                b, h = divmod(i, GH)
                if h == 0:
                    pe.wait_ge(s[f"kv_in{b}"], (n + 1) * (16 * CH))
                pe.wait_ge(s["kt_sb"], n * PAIRS + i)
                for c in range(CH):
                    ins = nc.tensor.transpose(bank(KT)[:, P * c:P * (c + 1)], kv[:, b, c, D * h:D * (h + 1)], ident[:])
                ins.then_inc(s["kt_psum"], 1)

            def queries(n, first=False):
                pe.wait_ge(s["ab_done"], n + 1)
                pe.wait_ge(s["v_sb"], n + 1)
                for j in range(REP):
                    ins = nc.tensor.transpose(bank(MA)[:, P * j:P * (j + 1)], qrope[:, j, :], ident[:])
                ins.then_inc(s["qt_psum"], 1)
                if not first:
                    pe.wait_ge(s["ot_sb"], 2 * n - 1)
                for j in range(REP):
                    ins = nc.tensor.transpose(bank(MB)[:, P * j:P * (j + 1)], qrope[:, REP + j, :], ident[:])
                ins.then_inc(s["qt_psum"], 1)

            def new_keys(n):
                pe.wait_ge(s["qt_sb_a"], n + 1)
                for h in range(GH):
                    ins = nc.tensor.transpose(bank(MA)[:, P * h:P * (h + 1)], qrope[:, QH + h, :], ident[:])
                ins.then_inc(s["kn_psum"], 1)

            for part in range(3):
                project(0, part, True)
            pe.wait_ge(s["consts_in"], 16)
            queries(0, True)
            keys(0, 0)
            new_keys(0)

            def transpose_probs(n, j):
                pe.wait_ge(s["p_sb"], n * PAIRS + (j + 1))
                pe.wait_ge(s["pt_sb"], n * PAIRS + j)
                for c in range(CH + 1):
                    ins = nc.tensor.transpose(psum[:, 512 * PT + P * c:512 * PT + P * (c + 1)],
                                              probs[:, j % 2, P * c:P * (c + 1)], ident[:])
                ins.then_inc(s["pt_psum"], 1)

            def values(n, j):
                b, h = divmod(j, GH)
                if j == 0:
                    pe.wait_ge(s["vnew_in"], (n + 1) * (16 * BT))
                if j % HALF == 0:
                    pe.wait_ge(s["o_sb"], 2 * n + j // HALF)
                pe.wait_ge(s["pt_sb"], n * PAIRS + (j + 1))
                for c in range(CH + 1):
                    vals = kv[:, b, c, D * (GH + h):D * (GH + h + 1)] if c < CH else v_new[:, b, D * h:D * (h + 1)]
                    ins = mm(bank(O)[:, D * (j % HALF):D * (j % HALF + 1)], pT[:, j % 2, P * c:P * (c + 1)], vals,
                             start=(c == 0), stop=(c == CH))
                    if h == GH - 1 and c == CH - 1:
                        ins.then_inc(s[f"kv_used{b}"], 1)
                ins.then_inc(s["pv_done"], 1)

            def round_(n, last, first=False):
                for i in range(PAIRS + 2):
                    if i + 1 < PAIRS:
                        keys(n, i + 1)
                    if i < PAIRS:
                        b, h = divmod(i, GH)
                        if i == 0:
                            pe.wait_ge(s["kn_sb"], n + 1)
                            pe.wait_ge(s["qt_sb_v"], n + 1)
                        pe.wait_ge(s["kt_sb"], n * PAIRS + (i + 1))
                        pe.wait_ge(s["s_done"], n * PAIRS + i)
                        mm(bank(SC), qT[:, h, b, :], kT[:, i % 2, :], start=True, stop=True)
                        mm(bank(SC + 1, S), qT[:, h, b, :], kT_new[:, h, S * b:S * (b + 1)],
                           start=True, stop=True).then_inc(s["s_psum"], 1)
                    if 1 <= i < PAIRS:
                        transpose_probs(n, i - 1)
                    if i >= 2:
                        values(n, i - 2)
                    if i == PAIRS:
                        transpose_probs(n, PAIRS - 1)
                        if not last:
                            queries(n + 1)
                    if i == 0 and not first:
                        output_projection(n - 1)
                    if i in (1, 2, 3) and not last:
                        project(n + 1, i - 1, False) if not first else project(1, i - 1, False, True)
                    if i == 6:
                        if not last:
                            pe.wait_ge(s["raw_v"], n + 2)
                        outputs(n, 0)
                if not last:
                    keys(n + 1, 0)
                    new_keys(n + 1)
                outputs(n, 1, last)

            def output_projection(n):
                pe.wait_ge(s["ot_sb"], 2 * n + 2)
                pe.wait_ge(s["wo_lo_done"], (n // TILES + 1) * (WO_PARTS * HALVES))
                for h in range(QH):
                    o_hi, o_lo = (part[:, h].rearrange("p b s -> p (b s)") for part in (oT_hi, oT_lo))
                    mm(bank(MB), o_hi, wo_hi[:, h, :], start=(h == 0), stop=False)
                    mm(bank(MB), o_hi, wo_lo[:, h, :], start=False, stop=False)
                    ins = mm(bank(MB), o_lo, wo_hi[:, h, :], start=False, stop=(h == QH - 1))
                ins.then_inc(s["wo_psum"], 1)

            def outputs(n, half, last=False):
                pe.wait_ge(s["o_sb"], 2 * n + (half + 1))
                if half and not last:
                    pe.wait_ge(s["qt_sb_v"], n + 2)
                elif half:
                    pe.wait_ge(s["ot_sb"], 2 * n + 1)
                for j in range(HALF):
                    ins = nc.tensor.transpose(bank(MB)[:, P * j:P * (j + 1)], o_nat[:, j, :], ident[:])
                ins.then_inc(s["ot_psum"], 1)

            round_(0, False, True)
            with pe.Fori(1, ROUNDS - 1) as n:
                round_(n, False)
            round_(ROUNDS - 1, True)
            output_projection(ROUNDS - 1)

            pe.wait_ge(s["wdone"], 1)
            pe.wait_ge(s["pt_sb"], ROUNDS * PAIRS)
            pe.wait_ge(s["o_sb"], 2 * ROUNDS)
            mm(bank(5), wb, bq_f, start=True, stop=True).then_inc(s["bq_psum"], 1)
            with pe.Fori(0, WAVES) as w:
                for j in range(WAVE):
                    if j == 0:
                        pe.wait_ge(s["x1_in"], w * 16 + 16)
                    if j >= 2:
                        pe.wait_ge(s["f_x2s"], w * WAVE + (j - 1))
                    for k in range(KC):
                        ins = mm(bank(j % 2)[:, P * k:P * (k + 1)], x1_now[:, j, P * k:P * (k + 1)],
                                 mix[:, bass.ds(w * WAVE + j, 1), :].rearrange("p a n -> p (a n)"), start=True, stop=True)
                    ins.then_inc(s["f_x2p"], 1)
                pe.wait_ge(s["tail_p"], TAIL_STEPS)
                for j in range(WAVE):
                    pe.wait_ge(s["f_x2s"], w * WAVE + (j + 1))
                    if j >= 2:
                        pe.wait_ge(s["f_x3s"], w * WAVE + (j - 1))
                    for k in range(KC):
                        ins = mm(bank(2 + j % 2), x2T[:, j, k, :], wT[:, k, :], start=(k == 0), stop=(k == KC - 1))
                    ins.then_inc(s["f_x3p"], 1)
                for j in range(WAVE):
                    pe.wait_ge(s["f_x3s"], w * WAVE + (j + 1))
                    if j >= 2:
                        pe.wait_ge(s["f_x3ts"], w * WAVE + (j - 1))
                    for k in range(KC):
                        ins = nc.tensor.transpose(bank(4 + j % 2)[:, P * k:P * (k + 1)], x3[:, j, P * k:P * (k + 1)], ident[:])
                    ins.then_inc(s["f_x3tp"], 1)
                for j in range(WAVE):
                    pe.wait_ge(s["f_x3ts"], w * WAVE + (j + 1))
                    if j == 0:
                        pe.wait_ge(s["f_out"], w * WAVE)
                    for k in range(KC):
                        ins = mm(bank(6)[:, P * j:P * (j + 1)], bT[:, k, :], x3T[:, j, k, :], start=(k == 0), stop=(k == KC - 1))
                ins.then_inc(s["f_bxp"], 1)
                pe.wait_ge(s["f_bxs"], w + 1)
                for j in range(WAVE):
                    if j >= 2:
                        pe.wait_ge(s["f_out"], w * WAVE + (j - 1))
                    mm(bank(7 - j % 2), bx[:, j, :], aT, start=True, stop=True).then_inc(s["f_yp"], 1)


def kernel(x, itok_Bx16_0_63, itok_B_207_1644, itok_B_0_15, condB_scale, itok_Bx4096x4096_0_255, condB_wscale,
           itok_Bx4096_0_255, condB_bscale, itok_B_3_7, _lenS, L0_cond_Wq, L0_cond_Wk, L0_cond_Wv, L0_cond_Wo,
           L0_cond_q_norm_w, L0_cond_k_norm_w, L0_cond_k_cache, L0_cond_v_cache, L1_cond_weights, L2_cond_weight,
           L2_cond_bias, L3_cond_A, L3_cond_B):
    import concourse.bacc as bacc
    from concourse.bass_utils import run_bass_kernel_spmd

    def rep(a, n=P):
        return np.broadcast_to(np.asarray(a).reshape(1, -1), (n, np.asarray(a).size))

    def by_row(a):
        a = np.asarray(a).reshape(TILES, BT, 1, -1)
        return np.broadcast_to(a, (TILES, BT, S, a.shape[-1])).reshape(TILES, P, -1).transpose(1, 0, 2)

    def weights(w, heads):
        w = np.asarray(w).reshape(GROUPS, heads // GROUPS * D, KC, P)
        return w.transpose(0, 3, 2, 1)

    x, table = np.asarray(x), np.asarray(itok_Bx16_0_63)
    pages = np.broadcast_to(table.reshape(B, CH, P // PSIZE, 1), (B, CH, P // PSIZE, PSIZE)).reshape(B * CH, P).T

    def cache(c):
        return np.asarray(c).reshape(PAGES * PSIZE, GROUPS, GH * D).transpose(1, 0, 2)

    arrays = {
        **constants(),
        "tbl_rep": pages,
        "len_rep": rep(itok_B_207_1644),
        "pos_rep": by_row(itok_B_207_1644)[:, :, 0],
        "cond_rep": by_row(itok_B_0_15)[:, :, 0],
        "scale_rep": rep(condB_scale),
        "wscale_rep": rep(condB_wscale),
        "zp_rep": rep(_lenS),
        "q_norm_rep": rep(L0_cond_q_norm_w),
        "k_norm_rep": rep(L0_cond_k_norm_w),
        "x_nat": x.reshape(TILES, P, HID),
        "xT": x.reshape(TILES, P, KC, P).transpose(0, 3, 2, 1),
        "wqkv": np.concatenate([weights(L0_cond_Wq, HQ), weights(L0_cond_Wk, HK), weights(L0_cond_Wv, HK)], axis=3),
        "wo": np.asarray(L0_cond_Wo).reshape(HID, GROUPS, QH, D).transpose(1, 3, 2, 0),
        "kv": np.concatenate([cache(L0_cond_k_cache), cache(L0_cond_v_cache)], axis=2).reshape(GROUPS * PAGES * PSIZE, -1),
        "mix": np.asarray(L1_cond_weights).reshape(CONDS * S, S),
        "weightT": np.asarray(L2_cond_weight).reshape(HID, KC, P).transpose(2, 1, 0),
        "bias_rep": rep(L2_cond_bias),
        "wq": np.asarray(itok_Bx4096x4096_0_255).reshape(B, HID, KC, P).transpose(0, 3, 2, 1).reshape(B, P, KC * HID),
        "bq": np.asarray(itok_Bx4096_0_255),
        "scale_col": np.asarray(condB_scale).reshape(B, 1),
        "bscale_col": np.asarray(condB_bscale).reshape(B, 1),
        "A_all": np.asarray(L3_cond_A).transpose(0, 2, 1).reshape(NAD * RANK, HID),
        "B_all": np.asarray(L3_cond_B).reshape(NAD * RANK, KC, P).transpose(2, 1, 0),
        "aid_rep": rep(np.repeat(np.asarray(itok_B_3_7), S)),
    }
    arrays = {k: np.ascontiguousarray(a) for k, a in arrays.items()}
    nc = bacc.Bacc("TRN2", target_bir_lowering=False, num_devices=1)
    tensors = {k: nc.dram_tensor(k, a.shape, mybir.dt.from_np(a.dtype), kind="ExternalInput").ap() for k, a in arrays.items()}
    tensors["out"] = nc.dram_tensor("out", (TILES, P, HID), F32, kind="ExternalOutput").ap()
    tensors["stream"] = nc.dram_tensor("stream", (TILES, P, HID), F32, kind="Internal").ap()
    tensors["ropes"] = nc.dram_tensor("ropes", (P, TILES * 4 * D), F32, kind="Internal").ap()
    build(nc, tensors)
    r = run_bass_kernel_spmd(nc, [arrays], core_ids=[0])
    return r.results[0]["out"].reshape(B, S, HID)
```
